# Optimizing a Trainium2 kernel written in Bass

```python
import numpy as np
import jax
import jax.numpy as jnp

def _softmax(x, axis=-1):
    return jax.nn.softmax(x, axis=axis)

def _gelu(x):
    return jax.nn.gelu(x, approximate=True)

def _silu(x):
    return jax.nn.silu(x)

def _sigmoid(x):
    return jax.nn.sigmoid(x)

def _layernorm(x, axis=-1, eps=1e-05):
    m = jnp.mean(x, axis=axis, keepdims=True)
    v = jnp.var(x, axis=axis, keepdims=True)
    return (x - m) / jnp.sqrt(v + eps)

def _scatter_add(tgt, idx, src, axis=0):
    return tgt.at[idx].add(src)

def _segment_sum(src, seg, n):
    return jax.ops.segment_sum(src, seg, n)
kernel_name = 'mk_gnn_resnorm_d2_gnn_r8_c187a4'

def setup_inputs(seed: int=0):
    np.random.seed(seed)
    _w = jnp.asarray

    def _rec_inputs():
        import jax
        import jax.numpy as jnp
        _gk = jax.random.key(seed)
        x = -0.000202 + 1 * jax.random.normal(jax.random.fold_in(_gk, 1), (12500, 64), jnp.float32)
        src = jax.random.randint(jax.random.fold_in(_gk, 2), (200000,), 0, 12500, jnp.int32)
        dst = jax.random.randint(jax.random.fold_in(_gk, 3), (200000,), 0, 12500, jnp.int32)
        _o = jnp.argsort(dst, stable=True)
        src = src[_o]
        dst = dst[_o]
        edge_attr_16 = -5.3897e-05 + 0.999841 * jax.random.normal(jax.random.fold_in(_gk, 11), (200000, 16), jnp.float32)
        return (x, src, dst, edge_attr_16)
    x, src, dst, edge_attr_16 = _rec_inputs()

    def _L0_gnn_setup():
        import jax, jax.numpy as jnp
        import numpy as np
        N, E, D, ED, H, O = (12500, 200000, 64, 16, 64, 64)
        key = jax.random.key(seed)
        ks = jax.random.split(key, 8)
        fan_in = 2 * D + ED
        s = 1.0 / np.sqrt(fan_in)
        return {'x': jax.random.normal(ks[0], (N, D), dtype=jnp.float32), 'edge_attr': jax.random.normal(ks[1], (E, ED), dtype=jnp.float32), 'edge_index': jax.random.randint(ks[2], (2, E), 0, N, dtype=jnp.int32), 'W1': jax.random.normal(ks[3], (fan_in, H), dtype=jnp.float32) * s, 'b1': jnp.zeros((H,), dtype=jnp.float32), 'W2': jax.random.normal(ks[4], (2 * H + ED, H), dtype=jnp.float32) * s, 'b2': jnp.zeros((H,), dtype=jnp.float32), 'W3': jax.random.normal(ks[5], (2 * H + ED, O), dtype=jnp.float32) * s, 'b3': jnp.zeros((O,), dtype=jnp.float32)}
    _L0_gnn_all = _L0_gnn_setup()
    _L0_gnn_in = {k: v for k, v in _L0_gnn_all.items() if k in ('W1', 'b1', 'W2', 'b2', 'W3', 'b3')}
    del _L0_gnn_all

    def _L1_gnn_setup():
        import jax, jax.numpy as jnp
        import numpy as np
        N_NODES = 12500
        N_EDGES = 200000
        D = 64

        def _gcn_conv(x, W, b, src, dst, norm, n_nodes):
            h = x @ W
            msgs = h[src] * norm[:, None]
            out = jax.ops.segment_sum(msgs, dst, num_segments=n_nodes)
            return out + b
        key = jax.random.key(seed)
        ks = jax.random.split(key, 6)
        x = jax.random.normal(ks[0], (N_NODES, D), dtype=jnp.float32)
        edge_index = jax.random.randint(ks[1], (2, N_EDGES), 0, N_NODES, dtype=jnp.int64)
        W1 = jax.random.normal(ks[2], (D, D), dtype=jnp.float32) / np.sqrt(D)
        b1 = jax.random.normal(ks[3], (D,), dtype=jnp.float32) * 0.02
        W2 = jax.random.normal(ks[4], (D, D), dtype=jnp.float32) / np.sqrt(D)
        b2 = jax.random.normal(ks[5], (D,), dtype=jnp.float32) * 0.02
        return {'x': x, 'edge_index': edge_index, 'W1': W1, 'b1': b1, 'W2': W2, 'b2': b2}
    _L1_gnn_all = _L1_gnn_setup()
    _L1_gnn_in = {k: v for k, v in _L1_gnn_all.items() if k in ('W1', 'b1', 'W2', 'b2')}
    del _L1_gnn_all
    return {'x': x, 'src': src, 'dst': dst, 'edge_attr_16': edge_attr_16, 'L0_gnn_W1': _L0_gnn_in['W1'], 'L0_gnn_b1': _L0_gnn_in['b1'], 'L0_gnn_W2': _L0_gnn_in['W2'], 'L0_gnn_b2': _L0_gnn_in['b2'], 'L0_gnn_W3': _L0_gnn_in['W3'], 'L0_gnn_b3': _L0_gnn_in['b3'], 'L1_gnn_W1': _L1_gnn_in['W1'], 'L1_gnn_b1': _L1_gnn_in['b1'], 'L1_gnn_W2': _L1_gnn_in['W2'], 'L1_gnn_b2': _L1_gnn_in['b2']}

def reference(x, src, dst, edge_attr_16, L0_gnn_W1, L0_gnn_b1, L0_gnn_W2, L0_gnn_b2, L0_gnn_W3, L0_gnn_b3, L1_gnn_W1, L1_gnn_b1, L1_gnn_W2, L1_gnn_b2):
    import jax
    import jax.numpy as jnp

    def _L0_gnn_ref(x, edge_attr, edge_index, W1, b1, W2, b2, W3, b3):
        import jax, jax.numpy as jnp
        import numpy as np
        N, E, D, ED, H, O = (12500, 200000, 64, 16, 64, 64)
        src = edge_index[0]
        dst = edge_index[1]
        n_nodes = x.shape[0]

        def conv(h, W, b):
            m = jnp.concatenate([h[dst], h[src], edge_attr], axis=1) @ W + b
            return jax.ops.segment_sum(m, dst, num_segments=n_nodes)
        h = jax.nn.relu(conv(x, W1, b1))
        h = jax.nn.relu(conv(h, W2, b2))
        return conv(h, W3, b3)

    def _L1_gnn_ref(x, edge_index, W1, b1, W2, b2):
        import jax, jax.numpy as jnp
        import numpy as np
        N_NODES = 12500
        N_EDGES = 200000
        D = 64

        def _gcn_conv(x, W, b, src, dst, norm, n_nodes):
            h = x @ W
            msgs = h[src] * norm[:, None]
            out = jax.ops.segment_sum(msgs, dst, num_segments=n_nodes)
            return out + b
        n = x.shape[0]
        loop = jnp.arange(n, dtype=edge_index.dtype)
        src = jnp.concatenate([edge_index[0], loop])
        dst = jnp.concatenate([edge_index[1], loop])
        deg = jax.ops.segment_sum(jnp.ones_like(src, dtype=x.dtype), dst, num_segments=n)
        dinv = jax.lax.rsqrt(deg)
        norm = dinv[src] * dinv[dst]
        h = _gcn_conv(x, W1, b1, src, dst, norm, n)
        h = jax.nn.relu(h)
        out = _gcn_conv(h, W2, b2, src, dst, norm, n)
        return out
    edge_index = jnp.stack([src, dst])
    x = _layernorm(x + _L0_gnn_ref(x, edge_attr_16, edge_index, L0_gnn_W1, L0_gnn_b1, L0_gnn_W2, L0_gnn_b2, L0_gnn_W3, L0_gnn_b3), axis=-1)
    x = _layernorm(x + _L1_gnn_ref(x, edge_index, L1_gnn_W1, L1_gnn_b1, L1_gnn_W2, L1_gnn_b2), axis=-1)
    return x

_drawn_inputs = setup_inputs


def setup_inputs(seed=0):
    import zlib

    import numpy as np

    out = dict(_drawn_inputs(seed))
    spreads = {'L0_gnn_b1': (0.0, 0.1), 'L0_gnn_b2': (0.0, 0.575), 'L0_gnn_b3': (0.0, 2.0)}
    factors = {'L1_gnn_b1': 4.618, 'L1_gnn_b2': 3.348}
    for name, (base, spread) in spreads.items():
        noise = np.random.default_rng([zlib.crc32(name.encode()), seed]).standard_normal(out[name].shape)
        drawn = base * np.exp(spread * noise) if base else spread * noise
        out[name] = jnp.asarray(drawn.astype(out[name].dtype))
    for name, factor in factors.items():
        out[name] = (out[name] * factor).astype(out[name].dtype)
    return out
```

```python
from contextlib import ExitStack

import concourse.bass as bass
from concourse import mybir

F32 = mybir.dt.float32
I32 = mybir.dt.int32
ALU = mybir.AluOpType
ACT = mybir.ActivationFunctionType
AX = mybir.AxisListType

LAYERS = 5
LN1, GCN1, LN2 = 2, 3, 4


def bass_gnn_resnorm(nc, x, src, dst, edge_attr, W, b, out):
    N, D = x.shape
    E, ED = edge_attr.shape
    P = 128
    TILES = 8
    GROUP = TILES * P
    GROUPS = -(-E // GROUP)
    GROUPS += GROUPS % 2
    WINDOW = 128
    WINDOWS = -(-N // WINDOW)
    FULL = E // GROUP
    TAIL = (E - FULL * GROUP) // TILES
    assert FULL == GROUPS - 1 and TAIL * TILES + FULL * GROUP == E
    TURN = 112
    TURNS = 4
    BATCH = TURN * TURNS
    BATCHES = -(-N // BATCH)
    assert BATCHES % 2 == 0 and BATCH <= 512
    NODES = max(BATCHES * BATCH, N - 1 + WINDOW, WINDOWS * WINDOW)
    EXTRA = ED + 1
    HELD = D + EXTRA
    SLOT = 96
    EPS = 1e-5

    with ExitStack() as ctx:
        def sb(name, shape, dt=F32):
            return ctx.enter_context(nc.sbuf_tensor(name, shape, dt))

        def pb(name):
            return ctx.enter_context(nc.psum_tensor(name, [P, 512], F32))

        def sem(name):
            return ctx.enter_context(nc.semaphore(name))

        table_a = nc.dram_tensor("table_a", (BATCHES * BATCH, D), F32).ap()
        table_b = nc.dram_tensor("table_b", (BATCHES * BATCH, D), F32).ap()
        least_dram = nc.dram_tensor("least_dram", (1, GROUPS), F32).ap()
        wide_dram = nc.dram_tensor("wide_dram", (1, GROUPS), F32).ap()
        tables = [x, table_a, table_b, table_a, table_b]

        sums_own = sb("sums_own", [P, NODES])
        edge_deg = sb("edge_deg", [P, NODES])
        resid = sb("resid", [P, BATCHES * BATCH])
        src_all = sb("src_all", [P, GROUPS * TILES], I32)
        near = sb("near", [P, GROUPS, TILES])
        least_all = sb("least_all", [P, GROUPS])
        least_row = sb("least_row", [1, GROUPS], I32)
        wide_row = sb("wide_row", [1, GROUPS], I32)
        index = [sb(f"index{k}", [P, TILES], I32) for k in range(2)]
        gathered = sb("gathered", [P, 2, TILES, SLOT])
        edge_in = sb("edge_in", [P, 2, TILES * ED])
        onehot = sb("onehot", [P, 2, TILES, WINDOW])
        far = sb("far", [P, 2, TILES])
        far_onehot = sb("far_onehot", [P, TILES, WINDOW])
        count = sb("count", [P, WINDOW])
        count_far = sb("count_far", [P, WINDOW])
        count_i = sb("count_i", [P, P], I32)
        ident = sb("ident", [P, P])
        center = sb("center", [D, 2 * D])
        mean = sb("mean", [D, 2 * D])
        deg_row = sb("deg_row", [EXTRA, 2 * D])
        weights = sb("weights", [P, LAYERS, 2 * D])
        edge_w = sb("edge_w", [EXTRA, 3, 2 * D])
        bias = sb("bias", [P, 2])
        zeros = sb("zeros", [D, 1])
        shift = sb("shift", [P, 2])
        turned = sb("turned", [TURN, 2, TURNS, D])
        stages = sb("stages", [P, 3, 2, BATCH])
        r_stage, q_stage, d_stage = (stages[:, n, :, :] for n in range(3))
        h_stage = sb("h_stage", [D, 2, BATCH])
        by_group = resid[0:GROUPS // 2, 0:2 * GROUP].bitcast(I32)
        by_group_f = resid[0:GROUPS // 2, 2 * GROUP:4 * GROUP]
        bounds = resid[0:GROUPS // 2, 4 * GROUP:4 * GROUP + 6]
        dst_i = edge_deg[:, 0:GROUPS * TILES].bitcast(I32)
        dst_f = edge_deg[:, GROUPS * TILES:2 * GROUPS * TILES]
        x_in = stages[0:TURN, :, :, :].rearrange("p n k c -> p (n k c)")[:, 0:2 * TURNS * 2 * D]
        x_in = x_in.rearrange("p (k q h d) -> p k q h d", k=2, q=TURNS, h=2)
        row_f = h_stage[0:1, 0, 0:2 * GROUPS].rearrange("o (k g) -> o k g", k=2)

        window = [pb(f"window{k}") for k in range(2)]
        side = [pb(f"side{k}") for k in range(2)]
        conv = [pb(f"conv{k}") for k in range(2)]
        turn = [pb(f"turn{k}") for k in range(2)]

        names = ("src_in dst_in group_in weights_in const const_i cleared prep least_out least_in "
                 "near_ready index_ready edge_ready onehot_ready summed added group_done "
                 "far_onehot far_summed far_added x_turned resid_ready deg_ready conv_ready "
                 "own_ready cleared_sums result_ready centered squared variance dinv_ready "
                 "new_resid scaled turned_ready rows_ready row_done halves rstd_ready edge_added sums_done own_first far_prep deg_root var_root passages").split()
        S = {n: sem(n) for n in names}
        landed = [[sem(f"landed{k}_{j}") for j in range(TILES)] for k in range(2)]
        edge_landed = [sem(f"edge_landed{k}") for k in range(2)]
        x_landed = [sem(f"x_landed{k}") for k in range(2)]
        stored = [sem(f"stored{k}") for k in range(2)]

        def before(layer, layers=range(LAYERS)):
            return BATCHES * sum(1 for other in layers if other < layer)

        def reach(eng, s, value):
            if not (isinstance(value, int) and value <= 0):
                eng.wait_ge(s, value)

        def reach_alone(eng, s, value):
            if not (isinstance(value, int) and value <= 0):
                eng.wait_ge(s, value)
                if not isinstance(value, int):
                    eng.sem_inc(S["passages"], 1)

        def rounds(eng, body, start, stop):
            with eng.Fori(start, stop) as it:
                body(it)

        X_ROUNDS = BATCHES // 2
        SUM_ROUNDS = GROUPS // 2
        assert X_ROUNDS < SUM_ROUNDS

        block = ctx.enter_context(nc.Block())

        def cols(batch):
            return bass.ds(batch * BATCH, BATCH)

        @block.sync
        def _(sp):
            sp.wait_ge(S["cleared"], 3)
            full, tail = FULL * GROUP, TAIL
            for host, held, s in ((src, src_all, "src_in"), (dst, dst_i, "dst_in")):
                sp.dma_start(held[:, 0:FULL * TILES].rearrange("p (g j) -> p g j", j=TILES),
                             host[0:full].rearrange("(g p j) -> p g j", p=P, j=TILES)).then_inc(S[s], 16)
                sp.dma_start(held[0:tail, FULL * TILES:GROUPS * TILES],
                             host[full:E].rearrange("(p j) -> p j", j=TILES)).then_inc(S[s], 16)
            pairs = GROUPS // 2
            sp.dma_start(by_group[0:pairs - 1, :],
                         dst[0:(pairs - 1) * 2 * GROUP].rearrange("(p e) -> p e", p=pairs - 1)).then_inc(S["group_in"], 16)
            sp.dma_start(by_group[pairs - 1:pairs, 0:E - (pairs - 1) * 2 * GROUP],
                         dst[(pairs - 1) * 2 * GROUP:E].rearrange("(p e) -> p e", p=1)).then_inc(S["group_in"], 16)
            sp.wait_ge(S["prep"], 7)
            sp.dma_start(least_dram.rearrange("o (p k) -> (o p) k", k=2), bounds[:, 0:2]).then_inc(S["least_out"], 16)
            sp.dma_start(wide_dram.rearrange("o (p k) -> (o p) k", k=2), bounds[:, 4:6]).then_inc(S["least_out"], 16)
            sp.wait_ge(S["least_out"], 32)
            sp.dma_start(least_all[:, :], least_dram.to_broadcast((P, GROUPS))).then_inc(S["least_in"], 16)
            sp.dma_start(row_f[:, 0, :], least_dram).then_inc(S["least_in"], 16)
            sp.dma_start(row_f[:, 1, :], wide_dram).then_inc(S["least_in"], 16)

            n = 0
            for layer in range(LAYERS):
                for half in range(2):
                    c = slice(half * D, (half + 1) * D)
                    if layer < GCN1:
                        parts = ((weights[0:D, layer, c], W[layer][D:2 * D, :]),
                                 (weights[D:2 * D, layer, c], W[layer][0:D, :]),
                                 (edge_w[0:ED, layer, c], W[layer][2 * D:2 * D + ED, :]),
                                 (edge_w[ED:EXTRA, layer, c], b[layer].rearrange("(o d) -> o d", o=1)))
                    else:
                        parts = ((weights[0:D, layer, c], W[layer]), (weights[D:2 * D, layer, c], W[layer]),
                                 (bias[half * D:half * D + D, layer - GCN1:layer - GCN1 + 1],
                                  b[layer].rearrange("(d o) -> d o", o=1)))
                    for to, of in parts:
                        sp.dma_start(to, of).then_inc(S["weights_in"], 16)
                        n += 1
            assert n == WEIGHT_LOADS

            def attributes(g, k, rows):
                reach(sp, S["edge_ready"], g - 1)
                first = g * GROUP
                sp.dma_start(edge_in[0:rows, k, :],
                             edge_attr[bass.ds(first, rows * TILES), :].rearrange("(p j) d -> p (j d)", j=TILES)
                             ).then_inc(edge_landed[k], 16)

            def nodes_of(batch, k, count):
                reach(sp, S["x_turned"], batch - 1)
                whole, rest = divmod(count, TURN)
                for half in range(2):
                    of = x[bass.ds(batch * BATCH, whole * TURN), :].rearrange("(q p) d -> p q d", p=TURN)
                    sp.dma_start(x_in[:, k, 0:whole, half, :], of).then_inc(x_landed[k], 16)
                    if rest:
                        sp.dma_start(x_in[0:rest, k, whole, half, :], x[N - rest:N, :]).then_inc(x_landed[k], 16)

            def x_round(it):
                for k in range(2):
                    batch = it * 2 + k
                    nodes_of(batch, k, min(BATCH, N - batch * BATCH) if isinstance(it, int) else BATCH)
                    attributes(batch, k, P)

            def edge_round(it):
                for k in range(2):
                    g = it * 2 + k
                    attributes(g, k, TAIL if isinstance(it, int) and g == FULL else P)

            x_round(0)
            rounds(sp, x_round, 1, X_ROUNDS - 1)
            x_round(X_ROUNDS - 1)
            rounds(sp, edge_round, X_ROUNDS, SUM_ROUNDS - 1)
            edge_round(SUM_ROUNDS - 1)

            for layer in range(LAYERS):
                def store(it):
                    for k in range(2):
                        batch = it * 2 + k
                        reach(sp, S["rows_ready"], before(layer) + batch + 1)
                        if layer < LAYERS - 1:
                            to = tables[layer + 1][cols(batch), :].rearrange("(q p) d -> p q d", p=TURN)
                            sp.dma_start(to, turned[:, k, :, :]).then_inc(stored[k], 16)
                        elif not isinstance(it, int) or (batch + 1) * BATCH <= N:
                            to = out[cols(batch), :].rearrange("(q p) d -> p q d", p=TURN)
                            sp.dma_start(to, turned[:, k, :, :]).then_inc(stored[k], 16)
                        else:
                            whole = (N - batch * BATCH) // TURN
                            first = batch * BATCH
                            rest = N - first - whole * TURN
                            sp.dma_start(out[first:first + whole * TURN, :].rearrange("(q p) d -> p q d", p=TURN),
                                         turned[:, k, 0:whole, :]).then_inc(stored[k], 16)
                            sp.dma_start(out[N - rest:N, :], turned[0:rest, k, whole, :]).then_inc(stored[k], 16)

                rounds(sp, store, 0, BATCHES // 2 - 1)
                store(BATCHES // 2 - 1)
            sp.wait_ge(stored[0], 16 * LAYERS * BATCHES // 2)
            sp.wait_ge(stored[1], 16 * (LAYERS * BATCHES // 2 + 1))

        @block.gpsimd
        def _(pool):
            pool.memset(src_all[:, :], 0).then_inc(S["cleared"], 1)
            pool.iota(count_i[:, :], pattern=[[1, P]], base=0, channel_multiplier=0).then_inc(S["const_i"], 1)
            pool.wait_ge(S["const"], 1)
            pool.iota(count_i[:, :], pattern=[[1, P]], base=0, channel_multiplier=-1).then_inc(S["const_i"], 1)
            pool.wait_ge(S["const"], 2)
            pool.iota(count_i[0:D, :], pattern=[[0, 2], [1, D]], base=0, channel_multiplier=-1).then_inc(S["const_i"], 1)
            pool.wait_ge(S["const"], 3)
            pool.iota(count_i[0:EXTRA, :], pattern=[[0, P]], base=0, channel_multiplier=1).then_inc(S["const_i"], 1)

            for layer in range(LAYERS):
                first = layer * GROUPS
                if layer:
                    for k in range(2):
                        pool.wait_ge(stored[k], 16 * layer * BATCHES // 2)
                    pool.wait_ge(S["cleared_sums"], layer * BATCHES)
                    pool.wait_ge(S["own_ready"], layer * BATCHES)

                def gather(it):
                    for k in range(2):
                        reach_alone(pool, S["index_ready"], first + it * 2 + k + 1)
                        for j in range(TILES):
                            pool.indirect_dma_start(
                                out=gathered[:, k, j, 0:D], out_offset=None, in_=tables[layer],
                                in_offset=bass.IndirectOffsetOnAxis(ap=index[k][:, j:j + 1], axis=0),
                            ).then_inc(landed[k][j], 16)

                rounds(pool, gather, 0, SUM_ROUNDS)

                if layer < LAYERS - 1:
                    def clear(it):
                        for k in range(2):
                            batch = it * 2 + k
                            reach_alone(pool, S["conv_ready"], before(layer) + batch + 1)
                            pool.tensor_copy(sums_own[0:D, cols(batch)], zeros[:, :].to_broadcast((D, BATCH))).then_inc(S["cleared_sums"], 1)
                            if layer == LN1:
                                reach(pool, S["halves"], before(layer, (0, LN1, LN2)) + batch + 1)
                                reach_alone(pool, S["new_resid"], batch + 1)
                                pool.tensor_tensor(sums_own[D:2 * D, cols(batch)], resid[D:2 * D, cols(batch)],
                                                   edge_deg[D:2 * D, cols(batch)], ALU.mult).then_inc(S["own_ready"], 1)
                            if layer == GCN1:
                                reach_alone(pool, S["squared"], before(layer, (LN1, GCN1, LN2)) + batch + 1)
                                pool.tensor_tensor(sums_own[D:2 * D, cols(batch)], q_stage[D:2 * D, k, :],
                                                   edge_deg[D:2 * D, cols(batch)], ALU.mult).then_inc(S["own_ready"], 1)

                    rounds(pool, clear, 0, BATCHES // 2)

        @block.scalar
        def _(act):
            act.wait_ge(S["src_in"], 32)
            act.wait_ge(S["const"], 10)
            for layer in range(LAYERS):
                first = layer * GROUPS

                def feed(it):
                    for k in range(2):
                        g = it * 2 + k
                        reach_alone(act, S["group_done"], first + g - 1)
                        act.copy(index[k][:, :], src_all[:, bass.ds(g * TILES, TILES)]).then_inc(S["index_ready"], 1)
                        if layer == 0:
                            reach(act, edge_landed[k], it * 16 + 16)
                            act.copy(gathered[:, k, :, D:D + ED],
                                     edge_in[:, k, :].rearrange("p (j d) -> p j d", d=ED)).then_inc(S["edge_ready"], 1)

                feed(0)
                rounds(act, feed, 1, SUM_ROUNDS)

                def rows(it):
                    for k in range(2):
                        batch = it * 2 + k
                        n = before(layer) + batch
                        if layer < LN1:
                            reach(act, S["conv_ready"], n + 1)
                            reach(act, S["turned_ready"], n - 1)
                            act.activation(h_stage[:, k, :], conv[k][0:D, 0:BATCH], ACT.Relu).then_inc(S["result_ready"], 1)
                        if layer in (LN1, LN2):
                            reach(act, S["centered"], before(layer, (LN1, LN2)) + batch + 1)
                            reach(act, S["rstd_ready"], before(layer, (LN1, LN2)) + batch - 1)
                            act.activation(q_stage[0:D, k, :], window[k][0:D, 0:BATCH], ACT.Square).then_inc(S["squared"], 1)
                        if layer == LN1:
                            reach(act, S["result_ready"], n - 1)
                            reach(act, S["dinv_ready"], batch + 1)
                            act.activation(d_stage[:, k, :], conv[k][:, 0:BATCH], ACT.Sqrt,
                                           bias=shift[:, 0:1]).then_inc(S["deg_root"], 1)
                        if layer == GCN1:
                            reach(act, S["scaled"], before(layer, (LN1, GCN1, LN2)) + batch + 1)
                            reach(act, S["result_ready"], n - 1)
                            reach(act, S["own_ready"], n - 1)
                            act.activation(q_stage[:, k, :], r_stage[:, k, :], ACT.Relu,
                                           bias=bias[:, 0:1]).then_inc(S["squared"], 1)
                    if layer in (LN1, LN2):
                        for k in range(2):
                            reach(act, S["variance"], before(layer, (LN1, LN2)) + it * 2 + k + 1)
                            act.activation(q_stage[:, k, :], side[k][:, 0:BATCH], ACT.Sqrt,
                                           bias=shift[:, 1:2]).then_inc(S["var_root"], 1)
                    for k in range(2):
                        batch = it * 2 + k
                        n = before(layer) + batch
                        reach(act, S["turned_ready"], n + 1)
                        reach(act, stored[k], (layer * BATCHES // 2 + it) * 16)
                        act.copy(turned[:, k, :, :].rearrange("p q d -> p (q d)"),
                                 turn[k][0:TURN, 0:TURNS * D]).then_inc(S["rows_ready"], 1)

                act.wait_ge(S["weights_in"], 16 * WEIGHT_LOADS)
                rows(0)
                rounds(act, rows, 1, BATCHES // 2)

        @block.vector
        def _(dve):
            dve.memset(dst_i[:, :], -1).then_inc(S["cleared"], 1)
            dve.memset(by_group, -1).then_inc(S["cleared"], 1)
            dve.wait_ge(S["const_i"], 1)
            dve.tensor_copy(count[:, :], count_i[:, 0:WINDOW]).then_inc(S["const"], 1)
            dve.wait_ge(S["const_i"], 2)
            dve.tensor_scalar(ident[:, :], count_i[:, :], 0.0, None, ALU.is_equal).then_inc(S["const"], 1)
            dve.wait_ge(S["const_i"], 3)
            dve.tensor_scalar(center[:, :], count_i[0:D, :], 0.0, -1.0 / D, ALU.is_equal, ALU.add).then_inc(S["const"], 1)
            dve.wait_ge(S["const_i"], 4)
            dve.tensor_scalar(deg_row[:, :], count_i[0:EXTRA, :], float(ED), None, ALU.is_equal).then_inc(S["const"], 1)
            dve.memset(mean[:, :], 1.0 / D).then_inc(S["const"], 1)
            dve.memset(zeros[:, :], 0.0).then_inc(S["const"], 1)
            dve.memset(shift[:, 0:1], 1.0).then_inc(S["const"], 1)
            dve.memset(shift[:, 1:2], EPS).then_inc(S["const"], 1)
            dve.memset(gathered[:, :, :, D + ED:HELD], 1.0).then_inc(S["const"], 1)
            dve.memset(sums_own[:, :], 0.0).then_inc(S["const"], 1)

            pair = "p (k e) -> p k e"
            dve.wait_ge(S["group_in"], 32)
            dve.tensor_copy(by_group_f, by_group).then_inc(S["prep"], 1)
            dve.wait_ge(S["prep"], 1)
            dve.tensor_reduce(bounds[:, 2:4], by_group_f.rearrange(pair, k=2), AX.X, ALU.max).then_inc(S["prep"], 1)
            held = by_group.bitcast(F32)
            dve.tensor_scalar(held, by_group_f, 0.0, float(N), ALU.is_lt, ALU.mult).then_inc(S["prep"], 1)
            dve.wait_ge(S["prep"], 3)
            dve.tensor_tensor(held, held, by_group_f, ALU.add).then_inc(S["prep"], 1)
            dve.wait_ge(S["prep"], 4)
            dve.tensor_reduce(bounds[:, 0:2], held.rearrange(pair, k=2), AX.X, ALU.min).then_inc(S["prep"], 1)
            dve.wait_ge(S["prep"], 5)
            dve.tensor_tensor(bounds[:, 2:4], bounds[:, 2:4], bounds[:, 0:2], ALU.subtract).then_inc(S["prep"], 1)
            dve.wait_ge(S["prep"], 6)
            dve.tensor_scalar(bounds[:, 4:6], bounds[:, 2:4], float(WINDOW), None, ALU.is_ge).then_inc(S["prep"], 1)
            dve.wait_ge(S["least_in"], 48)
            dve.tensor_copy(least_row[:, :], row_f[:, 0, :]).then_inc(S["row_done"], 1)
            dve.tensor_copy(wide_row[:, :], row_f[:, 1, :]).then_inc(S["row_done"], 1)
            dve.wait_ge(S["dst_in"], 32)
            dve.tensor_copy(dst_f, dst_i).then_inc(S["near_ready"], 1)
            dve.wait_ge(S["near_ready"], 1)
            dve.tensor_tensor(near[:, :, :], dst_f.rearrange("p (g j) -> p g j", j=TILES),
                              least_all[:, :].unsqueeze(2).to_broadcast((P, GROUPS, TILES)),
                              ALU.subtract).then_inc(S["near_ready"], 1)
            dve.wait_ge(S["near_ready"], 2)
            dve.memset(edge_deg[:, :], 0.0).then_inc(S["near_ready"], 1)
            dve.wait_ge(S["near_ready"], 3)

            def of_group(targets, g):
                return targets[:, bass.ds(g, 1), :].rearrange("p o j -> p (o j)")

            def spread(targets):
                return targets.unsqueeze(2).to_broadcast((P, TILES, WINDOW))

            def each(row):
                return row.unsqueeze(1).to_broadcast((P, TILES, WINDOW))

            def take_x(batch, k):
                reach(dve, S["x_turned"], batch + 1)
                dve.tensor_scalar(resid[:, cols(batch)], conv[k][:, 0:BATCH], 0.0, None,
                                  ALU.add).then_inc(S["resid_ready"], 1)

            for layer in range(LAYERS):
                first = layer * GROUPS

                def build(g, k):
                    reach(dve, S["group_done"], first + g - 1)
                    dve.tensor_tensor(onehot[:, k, :, :], each(count[:, :]), spread(of_group(near, g)),
                                      ALU.is_equal).then_inc(S["onehot_ready"], 1)

                def add_at(bank, at, done, edge_done):
                    where = bass.ds(at, WINDOW)
                    dve.tensor_tensor(sums_own[0:D, where], bank[0:D, 0:WINDOW], sums_own[0:D, where],
                                      ALU.add).then_inc(done, 1)
                    if layer == 0:
                        dve.tensor_tensor(edge_deg[0:EXTRA, where], bank[D:HELD, 0:WINDOW],
                                          edge_deg[0:EXTRA, where], ALU.add).then_inc(edge_done, 1)

                def add(g, k):
                    reach(dve, S["summed"], first + g + 1)
                    reach(dve, S["added"], first + g)
                    if layer == 0:
                        reach(dve, S["edge_added"], g)
                    at = dve.value_load(least_row[0:1, bass.ds(g, 1)], min_val=0, max_val=N - 1)
                    add_at(window[k], at, S["added"], S["edge_added"])
                    wide = dve.value_load(wide_row[0:1, bass.ds(g, 1)], min_val=0, max_val=1)
                    with dve.If(wide > 0):
                        reach(dve, S["added"], first + g + 1)
                        if layer == 0:
                            reach(dve, S["edge_added"], g + 1)
                        dve.tensor_scalar(far[:, 0, :], of_group(near, g), least_all[:, bass.ds(g, 1)], 1.0,
                                          ALU.add, ALU.add).then_inc(S["far_prep"], 1)
                        dve.tensor_scalar(far[:, 1, :], of_group(near, g), float(WINDOW), None,
                                          ALU.is_ge).then_inc(S["far_prep"], 1)
                        dve.tensor_scalar(count_far[:, :], count[:, :], 1.0, None, ALU.add).then_inc(S["far_prep"], 1)
                        dve.wait_ge(S["far_prep"], 3)
                        dve.tensor_tensor(far[:, 0, :], far[:, 0, :], far[:, 1, :], ALU.mult).then_inc(S["far_prep"], 1)
                        dve.wait_ge(S["far_prep"], 4)
                        steps = 3 if layer == 0 else 2
                        dve.sem_inc(S["far_added"], steps)
                        with dve.Fori(0, WINDOWS) as w:
                            dve.wait_ge(S["far_added"], w * steps + steps)
                            dve.tensor_tensor(far_onehot[:, :, :], each(count_far[:, :]), spread(far[:, 0, :]),
                                              ALU.is_equal).then_inc(S["far_onehot"], 1)
                            dve.wait_ge(S["far_summed"], w + 1)
                            dve.tensor_scalar(count_far[:, :], count_far[:, :], float(WINDOW), None,
                                              ALU.add).then_inc(S["far_added"], 1)
                            add_at(side[0], w * WINDOW, S["far_added"], S["far_added"])
                        dve.wait_ge(S["far_added"], steps * (WINDOWS + 1))
                        reach(dve, S["group_done"], first + g + 1)
                        dve.sem_clear(S["far_added"])
                        dve.sem_clear(S["far_summed"])
                        dve.sem_clear(S["far_prep"])

                if layer:
                    dve.wait_ge(S["cleared_sums"], layer * BATCHES)

                def sum_round(it, with_x=False):
                    for k in range(2):
                        g = it * 2 + k
                        build(g, k)
                        if with_x:
                            take_x(g, k)
                        if not (isinstance(g, int) and g == 0):
                            add(g - 1, 1 - k)

                sum_round(0, with_x=layer == 0)
                if layer == 0:
                    rounds(dve, lambda it: sum_round(it, with_x=True), 1, X_ROUNDS)
                rounds(dve, sum_round, X_ROUNDS if layer == 0 else 1, SUM_ROUNDS)
                add(GROUPS - 1, 1)
                dve.wait_ge(S["added"], first + GROUPS)
                if layer == 0:
                    dve.wait_ge(S["edge_added"], GROUPS)
                dve.sem_inc(S["sums_done"], 1)

                def node(it):
                    ks = [(k, it * 2 + k) for k in range(2)]
                    if layer == 0:
                        for k, batch in ks:
                            reach(dve, S["deg_ready"], batch + 1)
                            dve.tensor_scalar(edge_deg[D:2 * D, cols(batch)], side[k][D:2 * D, 0:BATCH], 0.0, None,
                                              ALU.add).then_inc(S["halves"], 1)
                            dve.tensor_tensor(sums_own[D:2 * D, cols(batch)], side[k][D:2 * D, 0:BATCH],
                                              resid[D:2 * D, cols(batch)], ALU.mult).then_inc(S["own_first"], 1)
                            reach(dve, S["halves"], batch + 1)
                    for k, batch in ks:
                        n = before(layer) + batch
                        reach(dve, S["conv_ready"], n + 1)
                        if layer < LN1:
                            dve.scalar_tensor_tensor(out=sums_own[D:2 * D, cols(batch)], in0=conv[k][D:2 * D, 0:BATCH],
                                                     scalar=0.0, in1=edge_deg[D:2 * D, cols(batch)],
                                                     op0=ALU.max, op1=ALU.mult).then_inc(S["own_ready"], 1)
                        if layer in (LN1, LN2):
                            reach(dve, S["centered"], before(layer, (LN1, LN2)) + batch - 1)
                        if layer == LN1:
                            dve.tensor_tensor(r_stage[:, k, :], conv[k][:, 0:BATCH], resid[:, cols(batch)],
                                              ALU.add).then_inc(S["scaled"], 1)
                        if layer == GCN1:
                            reach(dve, S["squared"], before(layer, (LN1, GCN1, LN2)) + batch - 1)
                            dve.tensor_tensor(r_stage[:, k, :], conv[k][:, 0:BATCH], edge_deg[:, cols(batch)],
                                              ALU.mult).then_inc(S["scaled"], 1)
                        if layer == LN2:
                            dve.tensor_tensor(d_stage[:, k, :], conv[k][:, 0:BATCH], edge_deg[:, cols(batch)],
                                              ALU.mult).then_inc(S["halves"], 1)
                            reach(dve, S["halves"], before(layer, (0, LN1, LN2)) + batch + 1)
                            dve.scalar_tensor_tensor(out=r_stage[:, k, :], in0=d_stage[:, k, :], scalar=bias[:, 1:2],
                                                     in1=resid[:, cols(batch)], op0=ALU.add,
                                                     op1=ALU.add).then_inc(S["scaled"], 1)
                    if layer == LN1:
                        for k, batch in ks:
                            reach_alone(dve, S["deg_root"], batch + 1)
                            dve.reciprocal(edge_deg[:, cols(batch)], d_stage[:, k, :]).then_inc(S["halves"], 1)
                    for k, batch in ks:
                        n = before(layer) + batch
                        if layer in (LN1, LN2):
                            reach(dve, S["var_root"], before(layer, (LN1, LN2)) + batch + 1)
                            if layer == LN1:
                                reach(dve, S["halves"], before(layer, (0, LN1)) + batch + 1)
                            dve.reciprocal(d_stage[:, k, :], q_stage[:, k, :]).then_inc(S["rstd_ready"], 1)
                            reach(dve, S["rstd_ready"], before(layer, (LN1, LN2)) + batch + 1)
                        if layer == LN1:
                            dve.tensor_tensor(resid[:, cols(batch)], window[k][:, 0:BATCH], d_stage[:, k, :],
                                              ALU.mult).then_inc(S["new_resid"], 1)
                            reach(dve, S["new_resid"], batch + 1)
                            reach(dve, S["halves"], before(layer, (0, LN1, LN2)) + batch + 1)
                            reach(dve, S["turned_ready"], n - 1)
                            dve.tensor_tensor(h_stage[:, k, :], resid[0:D, cols(batch)], edge_deg[0:D, cols(batch)],
                                              ALU.mult).then_inc(S["result_ready"], 1)
                        if layer == GCN1:
                            reach(dve, S["squared"], before(layer, (LN1, GCN1, LN2)) + batch + 1)
                            reach(dve, S["turned_ready"], n - 1)
                            dve.tensor_tensor(h_stage[:, k, :], q_stage[0:D, k, :], edge_deg[0:D, cols(batch)],
                                              ALU.mult).then_inc(S["result_ready"], 1)
                        if layer == LN2:
                            reach(dve, S["turned_ready"], n - 1)
                            dve.tensor_tensor(h_stage[:, k, :], window[k][0:D, 0:BATCH], d_stage[0:D, k, :],
                                              ALU.mult).then_inc(S["result_ready"], 1)

                node(0)
                rounds(dve, node, 1, BATCHES // 2)

        @block.tensor
        def _(pe):
            pe.wait_ge(S["const"], 10)
            pe.wait_ge(S["row_done"], 2)

            def turn_x(it, batch, k):
                last = isinstance(it, int) and (batch + 1) * BATCH > N
                reach(pe, x_landed[k], it * 32 + (64 if last else 32))
                reach(pe, S["resid_ready"], batch - 1)
                for q in range(TURNS):
                    ins = pe.transpose(conv[k][:, q * TURN:(q + 1) * TURN],
                                       x_in[:, k, q, :, :].rearrange("p h d -> p (h d)"), ident[0:TURN, 0:TURN])
                ins.then_inc(S["x_turned"], 1)

            for layer in range(LAYERS):
                first = layer * GROUPS
                rows = HELD if layer == 0 else D

                def sum_round(it, with_x=False):
                    for k in range(2):
                        g = it * 2 + k
                        if with_x:
                            turn_x(it, g, k)
                        reach(pe, S["onehot_ready"], first + g + 1)
                        reach(pe, S["added"], first + g - 1)
                        if layer == 0:
                            reach(pe, S["edge_added"], g - 1)
                        if layer == 0:
                            reach(pe, S["edge_ready"], g + 1)
                        for j in range(TILES):
                            reach(pe, landed[k][j], (layer * GROUPS // 2 + it) * 16 + 16)
                            ins = pe.matmul(window[k][0:rows, 0:WINDOW], gathered[:, k, j, 0:rows],
                                            onehot[:, k, j, :], start=(j == 0), stop=(j == TILES - 1))
                        ins.then_inc(S["summed"], 1)
                        wide = pe.value_load(wide_row[0:1, bass.ds(g, 1)], min_val=0, max_val=1)
                        with pe.If(wide > 0):
                            with pe.Fori(0, WINDOWS) as w:
                                pe.wait_ge(S["far_onehot"], w + 1)
                                for j in range(TILES):
                                    ins = pe.matmul(side[0][0:rows, 0:WINDOW], gathered[:, k, j, 0:rows],
                                                    far_onehot[:, j, :], start=(j == 0), stop=(j == TILES - 1))
                                ins.then_inc(S["far_summed"], 1)
                            pe.wait_ge(S["far_summed"], WINDOWS)
                            pe.sem_clear(S["far_onehot"])
                        reach(pe, S["summed"], first + g + 1)
                        pe.sem_inc(S["group_done"], 1)

                sum_round(0, with_x=layer == 0)
                if layer == 0:
                    rounds(pe, lambda it: sum_round(it, with_x=True), 1, X_ROUNDS - 1)
                    sum_round(X_ROUNDS - 1, with_x=True)
                rounds(pe, sum_round, X_ROUNDS if layer == 0 else 1, SUM_ROUNDS)
                pe.wait_ge(S["weights_in"], 16 * WEIGHT_LOADS)
                pe.wait_ge(S["sums_done"], layer + 1)
                pe.wait_ge(S["resid_ready"], BATCHES)
                if layer:
                    pe.wait_ge(S["own_ready"], before(layer))
                    pe.wait_ge(S["result_ready"], before(layer))

                def node(it):
                    ks = [(k, it * 2 + k) for k in range(2)]
                    if layer == 0:
                        for k, batch in ks:
                            reach(pe, S["halves"], batch - 1)
                            reach_alone(pe, S["own_first"], batch - 1)
                            pe.matmul(side[k][:, 0:BATCH], deg_row[:, :], edge_deg[0:EXTRA, cols(batch)],
                                      start=True, stop=True).then_inc(S["deg_ready"], 1)
                    for k, batch in ks:
                        n = before(layer) + batch
                        if layer == 0:
                            reach(pe, S["own_first"], batch + 1)
                        if layer < LN1:
                            reach(pe, S["result_ready"], n - 1)
                            reach(pe, S["own_ready"], n - 1)
                        if layer == LN1:
                            reach(pe, S["halves"], before(layer, (0, LN1, LN2)) + batch - 1)
                        if layer in (GCN1, LN2):
                            reach(pe, S["scaled"], before(layer, (LN1, GCN1, LN2)) + batch - 1)
                        last = pe.matmul(conv[k][:, 0:BATCH], weights[:, layer, :], sums_own[:, cols(batch)],
                                         start=True, stop=(layer >= GCN1))
                        if layer < GCN1:
                            last = pe.matmul(conv[k][:, 0:BATCH], edge_w[:, layer, :], edge_deg[0:EXTRA, cols(batch)],
                                             start=False, stop=True)
                        last.then_inc(S["conv_ready"], 1)
                    if layer in (LN1, LN2):
                        for k, batch in ks:
                            m = before(layer, (LN1, LN2)) + batch
                            reach(pe, S["scaled"], before(layer, (LN1, GCN1, LN2)) + batch + 1)
                            reach(pe, S["result_ready"], before(layer) + batch - 1)
                            pe.matmul(window[k][:, 0:BATCH], center[:, :], r_stage[0:D, k, :],
                                      start=True, stop=True).then_inc(S["centered"], 1)
                            if layer == LN1:
                                pe.matmul(conv[k][:, 0:BATCH], deg_row[:, :], edge_deg[0:EXTRA, cols(batch)],
                                          start=True, stop=True).then_inc(S["dinv_ready"], 1)
                        for k, batch in ks:
                            m = before(layer, (LN1, LN2)) + batch
                            reach(pe, S["squared"], before(layer, (LN1, GCN1, LN2)) + batch + 1)
                            reach(pe, S["rstd_ready"], m - 1)
                            pe.matmul(side[k][:, 0:BATCH], mean[:, :], q_stage[0:D, k, :],
                                      start=True, stop=True).then_inc(S["variance"], 1)
                    for k, batch in ks:
                        n = before(layer) + batch
                        reach_alone(pe, S["result_ready"], n + 1)
                        reach_alone(pe, S["rows_ready"], n - 1)
                        for q in range(TURNS):
                            ins = pe.transpose(turn[k][0:TURN, q * D:(q + 1) * D], h_stage[:, k, q * TURN:(q + 1) * TURN],
                                               ident[0:D, 0:D])
                        ins.then_inc(S["turned_ready"], 1)

                node(0)
                rounds(pe, node, 1, BATCHES // 2)


WEIGHT_LOADS = 2 * (3 * 4 + 2 * 3)

_INS = ["x", "src", "dst", "edge_attr_16"] + [f"L0_gnn_{n}{i}" for i in (1, 2, 3) for n in "Wb"] \
    + [f"L1_gnn_{n}{i}" for i in (1, 2) for n in "Wb"]


def kernel(**inputs):
    import numpy as _np
    import concourse.bacc as _bacc
    from concourse import mybir as _mybir
    from concourse.bass_utils import run_bass_kernel_spmd as _run

    nc = _bacc.Bacc("TRN2", target_bir_lowering=False, num_devices=1)
    arrays, args = {}, []
    for name in _INS:
        a = _np.ascontiguousarray(inputs[name])
        arrays[f"in_{name}_dram"] = a
        args.append(nc.dram_tensor(f"in_{name}_dram", a.shape, _mybir.dt.from_np(a.dtype), kind="ExternalInput").ap())
    out = nc.dram_tensor("out_dram", inputs["x"].shape, _mybir.dt.float32, kind="ExternalOutput").ap()
    bass_gnn_resnorm(nc, *args[:4], args[4::2], args[5::2], out)
    r = _run(nc, [arrays], core_ids=[0])
    return r.results[0]["out_dram"]
```

```python
from contextlib import ExitStack

import concourse.bass as bass
from concourse import mybir

F32 = mybir.dt.float32
I32 = mybir.dt.int32
ALU = mybir.AluOpType
ACT = mybir.ActivationFunctionType
AX = mybir.AxisListType

LAYERS = 5
LN1, GCN1, LN2 = 2, 3, 4


def bass_gnn_resnorm(nc, x, src, dst, edge_attr, W, b, out):
    N, D = x.shape
    E, ED = edge_attr.shape
    P = 128
    TILES = 8
    GROUP = TILES * P
    GROUPS = -(-E // GROUP)
    GROUPS += GROUPS % 2
    WINDOW = 128
    WINDOWS = -(-N // WINDOW)
    FULL = E // GROUP
    TAIL = (E - FULL * GROUP) // TILES
    assert FULL == GROUPS - 1 and TAIL * TILES + FULL * GROUP == E
    TURN = 112
    TURNS = 4
    BATCH = TURN * TURNS
    BATCHES = -(-N // BATCH)
    assert BATCHES % 2 == 0 and BATCH <= 512
    NODES = max(BATCHES * BATCH, N - 1 + WINDOW, WINDOWS * WINDOW)
    EXTRA = ED + 1
    HELD = D + EXTRA
    SLOT = 96
    EPS = 1e-5

    with ExitStack() as ctx:
        def sb(name, shape, dt=F32):
            return ctx.enter_context(nc.sbuf_tensor(name, shape, dt))

        def pb(name):
            return ctx.enter_context(nc.psum_tensor(name, [P, 512], F32))

        def sem(name):
            return ctx.enter_context(nc.semaphore(name))

        table_a = nc.dram_tensor("table_a", (BATCHES * BATCH, D), F32).ap()
        table_b = nc.dram_tensor("table_b", (BATCHES * BATCH, D), F32).ap()
        least_dram = nc.dram_tensor("least_dram", (1, GROUPS), F32).ap()
        wide_dram = nc.dram_tensor("wide_dram", (1, GROUPS), F32).ap()
        tables = [x, table_a, table_b, table_a, table_b]

        sums_own = sb("sums_own", [P, NODES])
        edge_deg = sb("edge_deg", [P, NODES])
        resid = sb("resid", [P, BATCHES * BATCH])
        src_all = sb("src_all", [P, GROUPS * TILES], I32)
        near = sb("near", [P, GROUPS, TILES])
        least_all = sb("least_all", [P, GROUPS])
        least_row = sb("least_row", [1, GROUPS], I32)
        wide_row = sb("wide_row", [1, GROUPS], I32)
        uneven_f = sb("uneven_f", [1, 2])
        uneven = sb("uneven", [1, 1], I32)
        index = [sb(f"index{k}", [P, TILES], I32) for k in range(2)]
        gathered = sb("gathered", [P, 2, TILES, SLOT])
        edge_in = sb("edge_in", [P, 2, TILES * ED])
        onehot = sb("onehot", [P, 2, TILES, WINDOW])
        far = sb("far", [P, 2, TILES])
        far_onehot = sb("far_onehot", [P, TILES, WINDOW])
        count = sb("count", [P, WINDOW])
        count_far = sb("count_far", [P, WINDOW])
        count_i = sb("count_i", [P, P], I32)
        ident = sb("ident", [P, P])
        center = sb("center", [D, 2 * D])
        mean = sb("mean", [D, 2 * D])
        deg_row = sb("deg_row", [EXTRA, 2 * D])
        weights = sb("weights", [P, LAYERS, 2 * D])
        edge_w = sb("edge_w", [EXTRA, 3, 2 * D])
        bias = sb("bias", [P, 2])
        zeros = sb("zeros", [P, 1])
        shift = sb("shift", [P, 2])
        turned = sb("turned", [TURN, 2, TURNS, D])
        stages = sb("stages", [P, 3, 2, BATCH])
        r_stage, q_stage, d_stage = (stages[:, n, :, :] for n in range(3))
        h_stage = sb("h_stage", [D, 2, BATCH])
        by_group = resid[0:GROUPS // 2, 0:2 * GROUP].bitcast(I32)
        by_group_f = resid[0:GROUPS // 2, 2 * GROUP:4 * GROUP]
        bounds = resid[0:GROUPS // 2, 4 * GROUP:4 * GROUP + 6]
        dst_i = edge_deg[:, 0:GROUPS * TILES].bitcast(I32)
        dst_f = edge_deg[:, GROUPS * TILES:2 * GROUPS * TILES]
        x_in = stages[0:TURN, :, :, :].rearrange("p n k c -> p (n k c)")[:, 0:2 * TURNS * 2 * D]
        x_in = x_in.rearrange("p (k q h d) -> p k q h d", k=2, q=TURNS, h=2)
        row_f = h_stage[0:1, 0, 0:2 * GROUPS].rearrange("o (k g) -> o k g", k=2)
        floor_f = h_stage[0:1, 1, 0:GROUPS]

        window = [pb(f"window{k}") for k in range(2)]
        side = [pb(f"side{k}") for k in range(2)]
        conv = [pb(f"conv{k}") for k in range(2)]
        turn = [pb(f"turn{k}") for k in range(2)]

        names = ("src_in dst_in group_in weights_in const const_i cleared prep least_out least_in "
                 "near_ready index_ready edge_ready onehot_ready summed added group_done "
                 "far_onehot far_summed far_added x_turned resid_ready deg_ready conv_ready "
                 "own_ready cleared_sums result_ready centered squared variance dinv_ready "
                 "new_resid scaled turned_ready rows_ready row_done halves rstd_ready edge_added sums_done own_first far_prep deg_root var_root passages index_first uneven_ready floor zeroed").split()
        S = {n: sem(n) for n in names}
        landed = [[sem(f"landed{k}_{j}") for j in range(TILES)] for k in range(2)]
        edge_landed = [sem(f"edge_landed{k}") for k in range(2)]
        x_landed = [sem(f"x_landed{k}") for k in range(2)]
        stored = [sem(f"stored{k}") for k in range(2)]

        def before(layer, layers=range(LAYERS)):
            return BATCHES * sum(1 for other in layers if other < layer)

        def reach(eng, s, value):
            if not (isinstance(value, int) and value <= 0):
                eng.wait_ge(s, value)

        def reach_alone(eng, s, value):
            if not (isinstance(value, int) and value <= 0):
                eng.wait_ge(s, value)
                if not isinstance(value, int):
                    eng.sem_inc(S["passages"], 1)

        def rounds(eng, body, start, stop):
            with eng.Fori(start, stop) as it:
                body(it)

        PAIRS = GROUPS // 2
        STEPS = BATCHES // 2
        SLOTS = PAIRS // STEPS
        PER_ROUND = 2 * SLOTS
        assert PAIRS == STEPS * SLOTS and GROUPS == FULL + 1
        FIRST_STAGE = 2
        SLACK = 2 * FIRST_STAGE
        X_PER = BATCHES // PER_ROUND
        assert X_PER == 2

        def fresh(layer):
            return layer in (0, LN1)

        def propagate(eng, layer, groups, stages, opening=None):
            def round_of(r):
                for slot in range(SLOTS):
                    groups(r * SLOTS + slot)
                    if slot in stages:
                        stages[slot](r - 1)

            if opening is not False:
                (opening or groups)(0)
                rounds(eng, opening or groups, 1, SLOTS)
            if fresh(layer):
                round_of(1)
            rounds(eng, round_of, 2 if fresh(layer) else 1, STEPS)

        def whole_phase(eng, layer, stages):
            def step(it):
                for slot in sorted(stages):
                    stages[slot](it)

            step(0)
            rounds(eng, step, 1, STEPS)

        block = ctx.enter_context(nc.Block())

        def cols(batch):
            return bass.ds(batch * BATCH, BATCH)

        @block.sync
        def _(sp):
            for k in range(2):
                sp.dma_start(index[k][:, :], src[k * GROUP:(k + 1) * GROUP].rearrange("(p j) -> p j", p=P)
                             ).then_inc(S["index_first"], 16)
            sp.wait_ge(S["cleared"], 3)
            full, tail = FULL * GROUP, TAIL
            for host, held, s in ((src, src_all, "src_in"), (dst, dst_i, "dst_in")):
                sp.dma_start(held[:, 0:FULL * TILES].rearrange("p (g j) -> p g j", j=TILES),
                             host[0:full].rearrange("(g p j) -> p g j", p=P, j=TILES)).then_inc(S[s], 16)
                sp.dma_start(held[0:tail, FULL * TILES:GROUPS * TILES],
                             host[full:E].rearrange("(p j) -> p j", j=TILES)).then_inc(S[s], 16)
            pairs = GROUPS // 2
            sp.dma_start(by_group[0:pairs - 1, :],
                         dst[0:(pairs - 1) * 2 * GROUP].rearrange("(p e) -> p e", p=pairs - 1)).then_inc(S["group_in"], 16)
            sp.dma_start(by_group[pairs - 1:pairs, 0:E - (pairs - 1) * 2 * GROUP],
                         dst[(pairs - 1) * 2 * GROUP:E].rearrange("(p e) -> p e", p=1)).then_inc(S["group_in"], 16)
            sp.wait_ge(S["prep"], 7)
            sp.dma_start(least_dram.rearrange("o (p k) -> (o p) k", k=2), bounds[:, 0:2]).then_inc(S["least_out"], 16)
            sp.dma_start(wide_dram.rearrange("o (p k) -> (o p) k", k=2), bounds[:, 4:6]).then_inc(S["least_out"], 16)
            sp.wait_ge(S["least_out"], 32)
            sp.dma_start(least_all[:, :], least_dram.to_broadcast((P, GROUPS))).then_inc(S["least_in"], 16)
            sp.dma_start(row_f[:, 0, :], least_dram).then_inc(S["least_in"], 16)
            sp.dma_start(row_f[:, 1, :], wide_dram).then_inc(S["least_in"], 16)

            n = 0
            for layer in range(LAYERS):
                for half in range(2):
                    c = slice(half * D, (half + 1) * D)
                    if layer < GCN1:
                        parts = ((weights[0:D, layer, c], W[layer][D:2 * D, :]),
                                 (weights[D:2 * D, layer, c], W[layer][0:D, :]),
                                 (edge_w[0:ED, layer, c], W[layer][2 * D:2 * D + ED, :]),
                                 (edge_w[ED:EXTRA, layer, c], b[layer].rearrange("(o d) -> o d", o=1)))
                    else:
                        parts = ((weights[0:D, layer, c], W[layer]), (weights[D:2 * D, layer, c], W[layer]),
                                 (bias[half * D:half * D + D, layer - GCN1:layer - GCN1 + 1],
                                  b[layer].rearrange("(d o) -> d o", o=1)))
                    for to, of in parts:
                        sp.dma_start(to, of).then_inc(S["weights_in"], 16)
                        n += 1
            assert n == WEIGHT_LOADS

            def attributes(g, k, rows):
                reach(sp, S["edge_ready"], g - 1)
                first = g * GROUP
                sp.dma_start(edge_in[0:rows, k, :],
                             edge_attr[bass.ds(first, rows * TILES), :].rearrange("(p j) d -> p (j d)", j=TILES)
                             ).then_inc(edge_landed[k], 16)

            def nodes_of(pair, k, count):
                batch = pair * X_PER + k
                reach(sp, S["x_turned"], batch - 1)
                whole, rest = divmod(count, TURN)
                for half in range(2):
                    of = x[bass.ds(batch * BATCH, whole * TURN), :].rearrange("(q p) d -> p q d", p=TURN)
                    sp.dma_start(x_in[:, k, 0:whole, half, :], of).then_inc(x_landed[k], 16)
                    if rest:
                        sp.dma_start(x_in[0:rest, k, whole, half, :], x[N - rest:N, :]).then_inc(x_landed[k], 16)

            def edge_pair(pair, with_x=False):
                for k in range(2):
                    g = pair * 2 + k
                    if with_x:
                        for kk in range(X_PER):
                            ends = isinstance(pair, int)
                            nodes_of(g, kk, min(BATCH, N - (g * X_PER + kk) * BATCH) if ends else BATCH)
                    attributes(g, k, TAIL if isinstance(pair, int) and g == FULL else P)

            def stores(layer):
                def store(it):
                    for k in range(2):
                        batch = it * 2 + k
                        reach(sp, S["rows_ready"], before(layer) + batch + 1)
                        if layer < LAYERS - 1:
                            to = tables[layer + 1][cols(batch), :].rearrange("(q p) d -> p q d", p=TURN)
                            sp.dma_start(to, turned[:, k, :, :]).then_inc(stored[k], 16)
                        elif not isinstance(it, int) or (batch + 1) * BATCH <= N:
                            to = out[cols(batch), :].rearrange("(q p) d -> p q d", p=TURN)
                            sp.dma_start(to, turned[:, k, :, :]).then_inc(stored[k], 16)
                        else:
                            whole = (N - batch * BATCH) // TURN
                            first = batch * BATCH
                            rest = N - first - whole * TURN
                            sp.dma_start(out[first:first + whole * TURN, :].rearrange("(q p) d -> p q d", p=TURN),
                                         turned[:, k, 0:whole, :]).then_inc(stored[k], 16)
                            sp.dma_start(out[N - rest:N, :], turned[0:rest, k, whole, :]).then_inc(stored[k], 16)
                return store

            edge_pair(0, with_x=True)
            rounds(sp, lambda pair: edge_pair(pair, with_x=True), 1, SLOTS - 1)
            edge_pair(SLOTS - 1, with_x=True)
            sp.wait_ge(S["uneven_ready"], 1)
            is_uneven = sp.value_load(uneven[0:1, 0:1], min_val=0, max_val=1)
            with sp.If(is_uneven > 0):
                rounds(sp, edge_pair, SLOTS, PAIRS - 1)
                edge_pair(PAIRS - 1)
                rounds(sp, stores(0), 0, STEPS)
            with sp.If(is_uneven < 1):
                def stored_round(r):
                    for slot in range(SLOTS):
                        edge_pair(r * SLOTS + slot)
                    stores(0)(r - 1)

                rounds(sp, stored_round, 1, STEPS - 1)
                stored_round(STEPS - 1)
                stores(0)(STEPS - 1)
            for layer in range(1, LAYERS):
                rounds(sp, stores(layer), 0, STEPS - 1)
                stores(layer)(STEPS - 1)
            sp.wait_ge(stored[0], 16 * LAYERS * BATCHES // 2)
            sp.wait_ge(stored[1], 16 * (LAYERS * BATCHES // 2 + 1))

        @block.gpsimd
        def _(pool):
            pool.memset(src_all[:, FULL * TILES:GROUPS * TILES], 0).then_inc(S["cleared"], 1)
            pool.iota(count_i[:, :], pattern=[[1, P]], base=0, channel_multiplier=0).then_inc(S["const_i"], 1)
            pool.wait_ge(S["const"], 2)
            pool.iota(count_i[:, :], pattern=[[1, P]], base=0, channel_multiplier=-1).then_inc(S["const_i"], 1)
            pool.wait_ge(S["const"], 3)
            pool.iota(count_i[0:D, :], pattern=[[0, 2], [1, D]], base=0, channel_multiplier=-1).then_inc(S["const_i"], 1)
            pool.wait_ge(S["const"], 4)
            pool.iota(count_i[0:EXTRA, :], pattern=[[0, P]], base=0, channel_multiplier=1).then_inc(S["const_i"], 1)

            for layer in range(LAYERS):
                first = layer * GROUPS
                if layer:
                    for k in range(2):
                        pool.wait_ge(stored[k], 16 * layer * BATCHES // 2)

                def gather(pair, indexed=None):
                    for k in range(2):
                        if indexed is None:
                            reach_alone(pool, S["index_ready"], first + pair * 2 + k - 1)
                        for j in range(TILES):
                            pool.indirect_dma_start(
                                out=gathered[:, k, j, 0:D], out_offset=None, in_=tables[layer],
                                in_offset=bass.IndirectOffsetOnAxis(ap=index[k][:, j:j + 1], axis=0),
                            ).then_inc(landed[k][j], 16)

                if layer == 0:
                    pool.wait_ge(S["index_first"], 32)
                    gather(0, indexed=True)
                rounds(pool, gather, 0 if layer else 1, PAIRS)

        @block.scalar
        def _(act):
            def feed(layer, spent, pair):
                for k in range(2):
                    g = pair * 2 + k
                    if not (layer == 0 and isinstance(pair, int) and pair == 0):
                        reach_alone(act, spent, layer * GROUPS + g - 1)
                        act.copy(index[k][:, :], src_all[:, bass.ds(g * TILES, TILES)]).then_inc(S["index_ready"], 1)
                    if layer == 0:
                        reach(act, edge_landed[k], pair * 16 + 16)
                        act.copy(gathered[:, k, :, D:D + ED],
                                 edge_in[:, k, :].rearrange("p (j d) -> p j d", d=ED)).then_inc(S["edge_ready"], 1)

            def stages(layer):
                ln = before(layer, (LN1, LN2))
                sq = before(layer, (LN1, GCN1, LN2))

                def clear_sums(it):
                    for k in range(2):
                        batch = it * 2 + k
                        reach_alone(act, S["conv_ready"], before(layer) + batch + 1)
                        act.copy(sums_own[0:D, cols(batch)], zeros[0:D, :].to_broadcast((D, BATCH))
                                 ).then_inc(S["cleared_sums"], 1)

                def relu(it):
                    for k in range(2):
                        n = before(layer) + it * 2 + k
                        reach(act, S["conv_ready"], n + 1)
                        reach(act, S["turned_ready"], n - 1)
                        act.activation(h_stage[:, k, :], conv[k][0:D, 0:BATCH], ACT.Relu).then_inc(S["result_ready"], 1)
                    clear_sums(it)

                def square(it):
                    for k in range(2):
                        batch = it * 2 + k
                        reach(act, S["centered"], ln + batch + 1)
                        reach(act, S["rstd_ready"], ln + batch - 1)
                        act.activation(q_stage[0:D, k, :], conv[k][0:D, 0:BATCH],
                                       ACT.Square).then_inc(S["squared"], 1)

                def degree_root(it):
                    for k in range(2):
                        batch = it * 2 + k
                        reach(act, S["result_ready"], before(layer) + batch - 1)
                        reach(act, S["dinv_ready"], batch + 1)
                        act.activation(d_stage[:, k, :], side[k][:, 0:BATCH], ACT.Sqrt,
                                       bias=shift[:, 0:1]).then_inc(S["deg_root"], 1)

                def deviation(it):
                    for k in range(2):
                        reach(act, S["variance"], ln + it * 2 + k + 1)
                        act.activation(q_stage[:, k, :], side[k][:, 0:BATCH], ACT.Sqrt,
                                       bias=shift[:, 1:2]).then_inc(S["var_root"], 1)

                def gcn_relu(it):
                    for k in range(2):
                        batch = it * 2 + k
                        reach(act, S["scaled"], sq + batch + 1)
                        reach(act, S["result_ready"], before(layer) + batch - 1)
                        reach(act, S["own_ready"], before(layer) + batch - 1)
                        act.activation(q_stage[:, k, :], r_stage[:, k, :], ACT.Relu,
                                       bias=bias[:, 0:1]).then_inc(S["squared"], 1)

                def rows(it):
                    for k in range(2):
                        reach(act, S["turned_ready"], before(layer) + it * 2 + k + 1)
                        reach(act, stored[k], (layer * STEPS + it) * 16)
                        act.copy(turned[:, k, :, :].rearrange("p q d -> p (q d)"),
                                 turn[k][0:TURN, 0:TURNS * D]).then_inc(S["rows_ready"], 1)

                def square_and_root(it):
                    square(it)
                    degree_root(it)

                return {0: {4: relu, 5: rows},
                        1: {3: relu, 4: rows},
                        LN1: {3: clear_sums, 4: square_and_root, 5: deviation, 6: rows},
                        GCN1: {3: clear_sums, 4: gcn_relu, 5: rows},
                        LN2: {4: square, 5: deviation, 6: rows}}[layer]

            act.wait_ge(S["const"], 1)
            act.copy(sums_own[:, :], zeros[:, :].to_broadcast((P, NODES))).then_inc(S["zeroed"], 1)
            act.wait_ge(S["src_in"], 32)
            act.wait_ge(S["const"], 9)
            feed(0, S["summed"], 0)
            act.wait_ge(S["near_ready"], 2)
            act.copy(edge_deg[:, :], zeros[:, :].to_broadcast((P, NODES))).then_inc(S["zeroed"], 1)
            act.wait_ge(S["uneven_ready"], 1)
            act.wait_ge(S["weights_in"], 16 * WEIGHT_LOADS)
            is_uneven = act.value_load(uneven[0:1, 0:1], min_val=0, max_val=1)
            with act.If(is_uneven > 0):
                for layer in range(LAYERS):
                    rounds(act, lambda pair: feed(layer, S["group_done"], pair), 0 if layer else 1, PAIRS)
                    whole_phase(act, layer, stages(layer))
            with act.If(is_uneven < 1):
                for layer in range(LAYERS):
                    if layer == 0:
                        rounds(act, lambda pair: feed(0, S["summed"], pair), 1, SLOTS)
                    propagate(act, layer, lambda pair: feed(layer, S["summed"], pair), stages(layer),
                              opening=False if layer == 0 else None)
                    for slot in sorted(stages(layer)):
                        stages(layer)[slot](STEPS - 1)

        @block.vector
        def _(dve):
            dve.memset(dst_i[:, FULL * TILES:GROUPS * TILES], -1).then_inc(S["cleared"], 1)
            dve.memset(by_group[96:GROUPS // 2, :], -1).then_inc(S["cleared"], 1)
            dve.memset(zeros[:, :], 0.0).then_inc(S["const"], 1)
            dve.wait_ge(S["const_i"], 1)
            dve.tensor_copy(count[:, :], count_i[:, 0:WINDOW]).then_inc(S["const"], 1)
            dve.wait_ge(S["const_i"], 2)
            dve.tensor_scalar(ident[:, :], count_i[:, :], 0.0, None, ALU.is_equal).then_inc(S["const"], 1)
            dve.wait_ge(S["const_i"], 3)
            dve.tensor_scalar(center[:, :], count_i[0:D, :], 0.0, -1.0 / D, ALU.is_equal, ALU.add).then_inc(S["const"], 1)
            dve.wait_ge(S["const_i"], 4)
            dve.tensor_scalar(deg_row[:, :], count_i[0:EXTRA, :], float(ED), None, ALU.is_equal).then_inc(S["const"], 1)
            dve.memset(mean[:, :], 1.0 / D).then_inc(S["const"], 1)
            dve.memset(shift[:, 0:1], 1.0).then_inc(S["const"], 1)
            dve.memset(shift[:, 1:2], EPS).then_inc(S["const"], 1)
            dve.memset(gathered[:, :, :, D + ED:HELD], 1.0).then_inc(S["const"], 1)
            for m in range(STEPS):
                part = floor_f[:, PER_ROUND * m + (SLACK if m else 0):min(GROUPS, PER_ROUND * (m + 1) + SLACK)]
                dve.memset(part, float(2 * BATCH * m)).then_inc(S["floor"], 1)

            pair = "p (k e) -> p k e"
            dve.wait_ge(S["group_in"], 32)
            dve.tensor_copy(by_group_f, by_group).then_inc(S["prep"], 1)
            dve.wait_ge(S["prep"], 1)
            dve.tensor_reduce(bounds[:, 2:4], by_group_f.rearrange(pair, k=2), AX.X, ALU.max).then_inc(S["prep"], 1)
            held = by_group.bitcast(F32)
            dve.tensor_scalar(held, by_group_f, 0.0, float(N), ALU.is_lt, ALU.mult).then_inc(S["prep"], 1)
            dve.wait_ge(S["prep"], 3)
            dve.tensor_tensor(held, held, by_group_f, ALU.add).then_inc(S["prep"], 1)
            dve.wait_ge(S["prep"], 4)
            dve.tensor_reduce(bounds[:, 0:2], held.rearrange(pair, k=2), AX.X, ALU.min).then_inc(S["prep"], 1)
            dve.wait_ge(S["prep"], 5)
            dve.tensor_tensor(bounds[:, 2:4], bounds[:, 2:4], bounds[:, 0:2], ALU.subtract).then_inc(S["prep"], 1)
            dve.wait_ge(S["prep"], 6)
            dve.tensor_scalar(bounds[:, 4:6], bounds[:, 2:4], float(WINDOW), None, ALU.is_ge).then_inc(S["prep"], 1)
            dve.wait_ge(S["dst_in"], 32)
            dve.tensor_copy(dst_f, dst_i).then_inc(S["near_ready"], 1)
            dve.wait_ge(S["near_ready"], 1)
            dve.wait_ge(S["least_in"], 48)
            dve.tensor_tensor(near[:, :, :], dst_f.rearrange("p (g j) -> p g j", j=TILES),
                              least_all[:, :].unsqueeze(2).to_broadcast((P, GROUPS, TILES)),
                              ALU.subtract).then_inc(S["near_ready"], 1)
            dve.tensor_copy(least_row[:, :], row_f[:, 0, :]).then_inc(S["row_done"], 1)
            dve.tensor_copy(wide_row[:, :], row_f[:, 1, :]).then_inc(S["row_done"], 1)
            dve.wait_ge(S["floor"], STEPS)
            dve.tensor_tensor(floor_f, row_f[:, 0, :], floor_f, ALU.is_lt).then_inc(S["floor"], 1)
            dve.tensor_reduce(uneven_f[:, 1:2], row_f[:, 1, :], AX.X, ALU.max).then_inc(S["floor"], 1)
            dve.wait_ge(S["floor"], STEPS + 2)
            dve.tensor_reduce(uneven_f[:, 0:1], floor_f, AX.X, ALU.max).then_inc(S["floor"], 1)
            dve.wait_ge(S["floor"], STEPS + 3)
            dve.tensor_reduce(uneven[:, :], uneven_f[:, :], AX.X, ALU.max).then_inc(S["uneven_ready"], 1)
            dve.wait_ge(S["near_ready"], 2)
            dve.wait_ge(S["row_done"], 2)

            def of_group(targets, g):
                return targets[:, bass.ds(g, 1), :].rearrange("p o j -> p (o j)")

            def spread(targets):
                return targets.unsqueeze(2).to_broadcast((P, TILES, WINDOW))

            def each(row):
                return row.unsqueeze(1).to_broadcast((P, TILES, WINDOW))

            def take_x(g):
                for k in range(X_PER):
                    batch = g * X_PER + k
                    reach(dve, S["x_turned"], batch + 1)
                    dve.tensor_scalar(resid[:, cols(batch)], conv[k][:, 0:BATCH], 0.0, None,
                                      ALU.add).then_inc(S["resid_ready"], 1)

            def build(layer, spent, g, k):
                reach(dve, spent, layer * GROUPS + g - 1)
                dve.tensor_tensor(onehot[:, k, :, :], each(count[:, :]), spread(of_group(near, g)),
                                  ALU.is_equal).then_inc(S["onehot_ready"], 1)

            def add_at(layer, bank, at, done, edge_done):
                where = bass.ds(at, WINDOW)
                dve.tensor_tensor(sums_own[0:D, where], bank[0:D, 0:WINDOW], sums_own[0:D, where],
                                  ALU.add).then_inc(done, 1)
                if layer == 0:
                    dve.tensor_tensor(edge_deg[0:EXTRA, where], bank[D:HELD, 0:WINDOW],
                                      edge_deg[0:EXTRA, where], ALU.add).then_inc(edge_done, 1)

            def add(layer, g, k):
                first = layer * GROUPS
                reach(dve, S["summed"], first + g + 1)
                reach(dve, S["added"], first + g)
                if layer == 0:
                    reach(dve, S["edge_added"], g)
                at = dve.value_load(least_row[0:1, bass.ds(g, 1)], min_val=0, max_val=N - 1)
                add_at(layer, window[k], at, S["added"], S["edge_added"])

            def add_far(layer, g):
                first = layer * GROUPS
                wide = dve.value_load(wide_row[0:1, bass.ds(g, 1)], min_val=0, max_val=1)
                with dve.If(wide > 0):
                    reach(dve, S["added"], first + g + 1)
                    if layer == 0:
                        reach(dve, S["edge_added"], g + 1)
                    dve.tensor_scalar(far[:, 0, :], of_group(near, g), least_all[:, bass.ds(g, 1)], 1.0,
                                      ALU.add, ALU.add).then_inc(S["far_prep"], 1)
                    dve.tensor_scalar(far[:, 1, :], of_group(near, g), float(WINDOW), None,
                                      ALU.is_ge).then_inc(S["far_prep"], 1)
                    dve.tensor_scalar(count_far[:, :], count[:, :], 1.0, None, ALU.add).then_inc(S["far_prep"], 1)
                    dve.wait_ge(S["far_prep"], 3)
                    dve.tensor_tensor(far[:, 0, :], far[:, 0, :], far[:, 1, :], ALU.mult).then_inc(S["far_prep"], 1)
                    dve.wait_ge(S["far_prep"], 4)
                    steps = 3 if layer == 0 else 2
                    dve.sem_inc(S["far_added"], steps)
                    with dve.Fori(0, WINDOWS) as w:
                        dve.wait_ge(S["far_added"], w * steps + steps)
                        dve.tensor_tensor(far_onehot[:, :, :], each(count_far[:, :]), spread(far[:, 0, :]),
                                          ALU.is_equal).then_inc(S["far_onehot"], 1)
                        dve.wait_ge(S["far_summed"], w + 1)
                        dve.tensor_scalar(count_far[:, :], count_far[:, :], float(WINDOW), None,
                                          ALU.add).then_inc(S["far_added"], 1)
                        add_at(layer, side[0], w * WINDOW, S["far_added"], S["far_added"])
                    dve.wait_ge(S["far_added"], steps * (WINDOWS + 1))
                    reach(dve, S["group_done"], first + g + 1)
                    dve.sem_clear(S["far_added"])
                    dve.sem_clear(S["far_summed"])
                    dve.sem_clear(S["far_prep"])

            def sums(layer, spent, pair, with_far=False, with_x=False):
                for k in range(2):
                    g = pair * 2 + k
                    build(layer, spent, g, k)
                    if with_x:
                        take_x(g)
                    if not (isinstance(g, int) and g == 0):
                        add(layer, g - 1, 1 - k)
                        if with_far:
                            add_far(layer, g - 1)

            def last_sums(layer, with_far=False):
                add(layer, GROUPS - 1, 1)
                if with_far:
                    add_far(layer, GROUPS - 1)
                dve.wait_ge(S["added"], (layer + 1) * GROUPS)
                if layer == 0:
                    dve.wait_ge(S["edge_added"], GROUPS)
                dve.sem_inc(S["sums_done"], 1)

            def stages(layer):
                base = before(layer)
                ln = before(layer, (LN1, LN2))
                sq = before(layer, (LN1, GCN1, LN2))
                half = before(layer, (0, LN1, LN2))

                def degrees(it):
                    for k in range(2):
                        batch = it * 2 + k
                        reach(dve, S["deg_ready"], batch + 1)
                        dve.tensor_scalar(edge_deg[D:2 * D, cols(batch)], side[k][D:2 * D, 0:BATCH], 0.0, None,
                                          ALU.add).then_inc(S["halves"], 1)
                        dve.tensor_tensor(sums_own[D:2 * D, cols(batch)], side[k][D:2 * D, 0:BATCH],
                                          resid[D:2 * D, cols(batch)], ALU.mult).then_inc(S["own_first"], 1)

                def own_next(it):
                    for k in range(2):
                        batch = it * 2 + k
                        reach(dve, S["conv_ready"], base + batch + 1)
                        reach(dve, S["halves"], batch + 1)
                        dve.scalar_tensor_tensor(out=sums_own[D:2 * D, cols(batch)], in0=conv[k][D:2 * D, 0:BATCH],
                                                 scalar=0.0, in1=edge_deg[D:2 * D, cols(batch)],
                                                 op0=ALU.max, op1=ALU.mult).then_inc(S["own_ready"], 1)

                def residual(it):
                    for k in range(2):
                        batch = it * 2 + k
                        reach(dve, S["conv_ready"], base + batch + 1)
                        reach(dve, S["centered"], ln + batch - 1)
                        dve.tensor_tensor(r_stage[:, k, :], conv[k][:, 0:BATCH], resid[:, cols(batch)],
                                          ALU.add).then_inc(S["scaled"], 1)

                def inverse_root(it):
                    for k in range(2):
                        batch = it * 2 + k
                        reach_alone(dve, S["deg_root"], batch + 1)
                        dve.reciprocal(edge_deg[:, cols(batch)], d_stage[:, k, :]).then_inc(S["halves"], 1)

                def norm(it, k):
                    batch = it * 2 + k
                    reach(dve, S["var_root"], ln + batch + 1)
                    if layer == LN1:
                        reach(dve, S["halves"], half + batch + 1)
                    dve.reciprocal(d_stage[:, k, :], q_stage[:, k, :]).then_inc(S["rstd_ready"], 1)
                    reach(dve, S["rstd_ready"], ln + batch + 1)

                def normalize(it):
                    for k in range(2):
                        batch = it * 2 + k
                        norm(it, k)
                        dve.tensor_tensor(resid[:, cols(batch)], conv[k][:, 0:BATCH], d_stage[:, k, :],
                                          ALU.mult).then_inc(S["new_resid"], 1)
                    for k in range(2):
                        batch = it * 2 + k
                        reach(dve, S["new_resid"], batch + 1)
                        reach(dve, S["turned_ready"], base + batch - 1)
                        dve.tensor_tensor(h_stage[:, k, :], resid[0:D, cols(batch)], edge_deg[0:D, cols(batch)],
                                          ALU.mult).then_inc(S["result_ready"], 1)
                        dve.tensor_tensor(sums_own[D:2 * D, cols(batch)], resid[D:2 * D, cols(batch)],
                                          edge_deg[D:2 * D, cols(batch)], ALU.mult).then_inc(S["own_ready"], 1)

                def scale(it):
                    for k in range(2):
                        batch = it * 2 + k
                        reach(dve, S["conv_ready"], base + batch + 1)
                        reach(dve, S["squared"], sq + batch - 1)
                        dve.tensor_tensor(r_stage[:, k, :], conv[k][:, 0:BATCH], edge_deg[:, cols(batch)],
                                          ALU.mult).then_inc(S["scaled"], 1)

                def gcn_result(it):
                    for k in range(2):
                        batch = it * 2 + k
                        reach(dve, S["squared"], sq + batch + 1)
                        reach(dve, S["turned_ready"], base + batch - 1)
                        dve.tensor_tensor(h_stage[:, k, :], q_stage[0:D, k, :], edge_deg[0:D, cols(batch)],
                                          ALU.mult).then_inc(S["result_ready"], 1)
                        dve.tensor_tensor(sums_own[D:2 * D, cols(batch)], q_stage[D:2 * D, k, :],
                                          edge_deg[D:2 * D, cols(batch)], ALU.mult).then_inc(S["own_ready"], 1)

                def scale_and_residual(it):
                    for k in range(2):
                        batch = it * 2 + k
                        reach(dve, S["conv_ready"], base + batch + 1)
                        reach(dve, S["centered"], ln + batch - 1)
                        dve.tensor_tensor(d_stage[:, k, :], conv[k][:, 0:BATCH], edge_deg[:, cols(batch)],
                                          ALU.mult).then_inc(S["halves"], 1)
                        reach(dve, S["halves"], half + batch + 1)
                        dve.scalar_tensor_tensor(out=r_stage[:, k, :], in0=d_stage[:, k, :], scalar=bias[:, 1:2],
                                                 in1=resid[:, cols(batch)], op0=ALU.add,
                                                 op1=ALU.add).then_inc(S["scaled"], 1)

                def last_result(it):
                    for k in range(2):
                        norm(it, k)
                        reach(dve, S["turned_ready"], base + it * 2 + k - 1)
                        dve.tensor_tensor(h_stage[:, k, :], conv[k][0:D, 0:BATCH], d_stage[0:D, k, :],
                                          ALU.mult).then_inc(S["result_ready"], 1)

                return {0: {3: degrees, 4: own_next},
                        1: {3: own_next},
                        LN1: {3: residual, 4: inverse_root, 5: normalize},
                        GCN1: {3: scale, 4: gcn_result},
                        LN2: {3: scale_and_residual, 5: last_result}}[layer]

            dve.wait_ge(S["uneven_ready"], 1)
            is_uneven = dve.value_load(uneven[0:1, 0:1], min_val=0, max_val=1)
            with dve.If(is_uneven > 0):
                dve.wait_ge(S["zeroed"], 2)
                for layer in range(LAYERS):
                    spent = S["group_done"]
                    if layer:
                        dve.wait_ge(S["cleared_sums"], layer * BATCHES)
                    sums(layer, spent, 0, with_far=True, with_x=layer == 0)
                    if layer == 0:
                        rounds(dve, lambda pair: sums(layer, spent, pair, with_far=True, with_x=True), 1, SLOTS)
                    rounds(dve, lambda pair: sums(layer, spent, pair, with_far=True), 1 if layer else SLOTS, PAIRS)
                    last_sums(layer, with_far=True)
                    whole_phase(dve, layer, stages(layer))
            with dve.If(is_uneven < 1):
                dve.wait_ge(S["zeroed"], 2)
                for layer in range(LAYERS):
                    if layer:
                        dve.wait_ge(S["cleared_sums"], layer * BATCHES)
                    propagate(dve, layer, lambda pair: sums(layer, S["summed"], pair), stages(layer),
                              opening=(lambda pair: sums(0, S["summed"], pair, with_x=True)) if layer == 0 else None)
                    last_sums(layer)
                    for slot in sorted(stages(layer)):
                        stages(layer)[slot](STEPS - 1)

        @block.tensor
        def _(pe):
            pe.wait_ge(S["const"], 9)
            pe.wait_ge(S["row_done"], 2)
            pe.wait_ge(S["uneven_ready"], 1)

            def turn_x(pair, k):
                g = pair * 2 + k
                for kk in range(X_PER):
                    batch = g * X_PER + kk
                    last = isinstance(g, int) and (batch + 1) * BATCH > N
                    reach(pe, x_landed[kk], g * 32 + (64 if last else 32))
                    reach(pe, S["resid_ready"], batch - 1)
                    for q in range(TURNS):
                        ins = pe.transpose(conv[kk][:, q * TURN:(q + 1) * TURN],
                                           x_in[:, kk, q, :, :].rearrange("p h d -> p (h d)"), ident[0:TURN, 0:TURN])
                    ins.then_inc(S["x_turned"], 1)

            def sum_far(layer, g, k):
                rows = HELD if layer == 0 else D
                wide = pe.value_load(wide_row[0:1, bass.ds(g, 1)], min_val=0, max_val=1)
                with pe.If(wide > 0):
                    with pe.Fori(0, WINDOWS) as w:
                        pe.wait_ge(S["far_onehot"], w + 1)
                        for j in range(TILES):
                            ins = pe.matmul(side[0][0:rows, 0:WINDOW], gathered[:, k, j, 0:rows],
                                            far_onehot[:, j, :], start=(j == 0), stop=(j == TILES - 1))
                        ins.then_inc(S["far_summed"], 1)
                    pe.wait_ge(S["far_summed"], WINDOWS)
                    pe.sem_clear(S["far_onehot"])
                reach(pe, S["summed"], layer * GROUPS + g + 1)
                pe.sem_inc(S["group_done"], 1)

            def sums(layer, pair, with_far=False, with_x=False):
                first = layer * GROUPS
                rows = HELD if layer == 0 else D
                for k in range(2):
                    g = pair * 2 + k
                    if with_x:
                        turn_x(pair, k)
                    reach(pe, S["onehot_ready"], first + g + 1)
                    reach(pe, S["added"], first + g - 1)
                    if layer == 0:
                        reach(pe, S["edge_added"], g - 1)
                        reach(pe, S["edge_ready"], g + 1)
                    for j in range(TILES):
                        reach(pe, landed[k][j], (layer * PAIRS + pair) * 16 + 16)
                        ins = pe.matmul(window[k][0:rows, 0:WINDOW], gathered[:, k, j, 0:rows],
                                        onehot[:, k, j, :], start=(j == 0), stop=(j == TILES - 1))
                    ins.then_inc(S["summed"], 1)
                    if with_far:
                        sum_far(layer, g, k)

            def stages(layer, gated=False):
                base = before(layer)
                ln = before(layer, (LN1, LN2))
                sq = before(layer, (LN1, GCN1, LN2))

                def gate(it):
                    if gated:
                        reach(pe, S["added"], layer * GROUPS + (it + 1) * PER_ROUND + SLACK)
                        if layer == 0:
                            reach(pe, S["edge_added"], (it + 1) * PER_ROUND + SLACK)

                def degrees(it):
                    gate(it)
                    for k in range(2):
                        batch = it * 2 + k
                        reach(pe, S["halves"], batch - 1)
                        reach_alone(pe, S["own_first"], batch - 1)
                        pe.matmul(side[k][:, 0:BATCH], deg_row[:, :], edge_deg[0:EXTRA, cols(batch)],
                                  start=True, stop=True).then_inc(S["deg_ready"], 1)

                def convolve(it):
                    if layer:
                        gate(it)
                    for k in range(2):
                        batch = it * 2 + k
                        if layer == 0:
                            reach(pe, S["own_first"], batch + 1)
                        if layer < LN1:
                            reach(pe, S["own_ready"], base + batch - 1)
                        if layer == GCN1:
                            reach(pe, S["scaled"], sq + batch - 1)
                        elif layer == LN1:
                            reach(pe, S["new_resid"], batch - 1)
                        else:
                            reach(pe, S["result_ready"], base + batch - 1)
                        last = pe.matmul(conv[k][:, 0:BATCH], weights[:, layer, :], sums_own[:, cols(batch)],
                                         start=True, stop=(layer >= GCN1))
                        if layer < GCN1:
                            last = pe.matmul(conv[k][:, 0:BATCH], edge_w[:, layer, :], edge_deg[0:EXTRA, cols(batch)],
                                             start=False, stop=True)
                        last.then_inc(S["conv_ready"], 1)

                def centre(it):
                    for k in range(2):
                        batch = it * 2 + k
                        reach(pe, S["scaled"], sq + batch + 1)
                        pe.matmul(conv[k][:, 0:BATCH], center[:, :], r_stage[0:D, k, :],
                                  start=True, stop=True).then_inc(S["centered"], 1)
                        if layer == LN1:
                            reach_alone(pe, S["var_root"], batch - 1)
                            pe.matmul(side[k][:, 0:BATCH], deg_row[:, :], edge_deg[0:EXTRA, cols(batch)],
                                      start=True, stop=True).then_inc(S["dinv_ready"], 1)

                def variance(it):
                    for k in range(2):
                        batch = it * 2 + k
                        reach(pe, S["squared"], sq + batch + 1)
                        reach(pe, S["var_root"], ln + batch - 1)
                        if layer == LN1:
                            reach(pe, S["deg_root"], batch + 1)
                        pe.matmul(side[k][:, 0:BATCH], mean[:, :], q_stage[0:D, k, :],
                                  start=True, stop=True).then_inc(S["variance"], 1)

                def turn_result(it):
                    for k in range(2):
                        n = base + it * 2 + k
                        reach_alone(pe, S["result_ready"], n + 1)
                        reach_alone(pe, S["rows_ready"], n - 1)
                        for q in range(TURNS):
                            ins = pe.transpose(turn[k][0:TURN, q * D:(q + 1) * D], h_stage[:, k, q * TURN:(q + 1) * TURN],
                                               ident[0:D, 0:D])
                        ins.then_inc(S["turned_ready"], 1)

                return {0: {2: degrees, 3: convolve, 4: turn_result},
                        1: {2: convolve, 3: turn_result},
                        LN1: {2: convolve, 3: centre, 4: variance, 5: turn_result},
                        GCN1: {2: convolve, 4: turn_result},
                        LN2: {2: convolve, 3: centre, 4: variance, 5: turn_result}}[layer]

            def ready(layer):
                pe.wait_ge(S["sums_done"], layer + 1)

            def opening(layer):
                if layer:
                    pe.wait_ge(S["own_ready"], before(layer))
                    pe.wait_ge(S["result_ready"], before(layer))

            is_uneven = pe.value_load(uneven[0:1, 0:1], min_val=0, max_val=1)
            with pe.If(is_uneven > 0):
                for layer in range(LAYERS):
                    opening(layer)
                    sums(layer, 0, with_far=True, with_x=layer == 0)
                    if layer == 0:
                        rounds(pe, lambda pair: sums(0, pair, with_far=True, with_x=True), 1, SLOTS - 1)
                        sums(0, SLOTS - 1, with_far=True, with_x=True)
                        pe.wait_ge(S["weights_in"], 16 * WEIGHT_LOADS)
                        pe.wait_ge(S["resid_ready"], BATCHES)
                    rounds(pe, lambda pair: sums(layer, pair, with_far=True), 1 if layer else SLOTS, PAIRS)
                    ready(layer)
                    whole_phase(pe, layer, stages(layer))
            with pe.If(is_uneven < 1):
                for layer in range(LAYERS):
                    opening(layer)
                    if layer == 0:
                        sums(0, 0, with_x=True)
                        rounds(pe, lambda pair: sums(0, pair, with_x=True), 1, SLOTS - 1)
                        sums(0, SLOTS - 1, with_x=True)
                        pe.wait_ge(S["weights_in"], 16 * WEIGHT_LOADS)
                        pe.wait_ge(S["resid_ready"], BATCHES)
                    propagate(pe, layer, lambda pair: sums(layer, pair), stages(layer, gated=True),
                              opening=False if layer == 0 else None)
                    ready(layer)
                    for slot, stage in sorted(stages(layer).items()):
                        stage(STEPS - 1)


WEIGHT_LOADS = 2 * (3 * 4 + 2 * 3)

_INS = ["x", "src", "dst", "edge_attr_16"] + [f"L0_gnn_{n}{i}" for i in (1, 2, 3) for n in "Wb"] \
    + [f"L1_gnn_{n}{i}" for i in (1, 2) for n in "Wb"]


def kernel(**inputs):
    import numpy as _np
    import concourse.bacc as _bacc
    from concourse import mybir as _mybir
    from concourse.bass_utils import run_bass_kernel_spmd as _run

    nc = _bacc.Bacc("TRN2", target_bir_lowering=False, num_devices=1)
    arrays, args = {}, []
    for name in _INS:
        a = _np.ascontiguousarray(inputs[name])
        arrays[f"in_{name}_dram"] = a
        args.append(nc.dram_tensor(f"in_{name}_dram", a.shape, _mybir.dt.from_np(a.dtype), kind="ExternalInput").ap())
    out = nc.dram_tensor("out_dram", inputs["x"].shape, _mybir.dt.float32, kind="ExternalOutput").ap()
    bass_gnn_resnorm(nc, *args[:4], args[4::2], args[5::2], out)
    r = _run(nc, [arrays], core_ids=[0])
    return r.results[0]["out_dram"]
```

```python
from contextlib import ExitStack

import concourse.bass as bass
from concourse import mybir

F32 = mybir.dt.float32
BF16 = mybir.dt.bfloat16
FP8 = mybir.dt.float8e4
U8 = mybir.dt.uint8
I32 = mybir.dt.int32
ALU = mybir.AluOpType
ACT = mybir.ActivationFunctionType
AX = mybir.AxisListType

LAYERS = 5
LN1, GCN1, LN2 = 2, 3, 4


def bass_gnn_resnorm(nc, x, src, dst, edge_attr, W, b, out):
    N, D = x.shape
    E, ED = edge_attr.shape
    P = 128
    TILES = 8
    GROUP = TILES * P
    GROUPS = -(-E // GROUP)
    GROUPS += GROUPS % 2
    WINDOW = 128
    WINDOWS = -(-N // WINDOW)
    FULL = E // GROUP
    TAIL = (E - FULL * GROUP) // TILES
    TURN = 112
    TURNS = 4
    BATCH = TURN * TURNS
    BATCHES = -(-N // BATCH)
    NODES = max(BATCHES * BATCH, N - 1 + WINDOW, WINDOWS * WINDOW)
    EXTRA = ED + 1
    PARTS = 3
    EPS = 1e-5

    DENSE = BATCHES // 2
    PER_ROUND = GROUPS // DENSE
    PER_BATCH = PER_ROUND // 2
    OPENING = 2
    SCATTERED = DENSE * PER_BATCH - OPENING
    LOOSE = GROUPS - SCATTERED
    ROUNDS = (LOOSE - OPENING) // PER_ROUND
    BLOCKS = -(-N // P)
    CHUNK = BLOCKS // PER_BATCH
    assert FULL == GROUPS - 1 and TAIL * TILES + FULL * GROUP == E
    assert BATCHES == 4 * ROUNDS and DENSE == 2 * ROUNDS and BLOCKS == CHUNK * PER_BATCH
    assert OPENING + ROUNDS * PER_ROUND == LOOSE and PER_ROUND % 2 == 0 and BLOCKS * P == BATCHES * BATCH
    LANE_BITS, BATCH_BITS = 16, 23
    LANE_USED = BLOCKS * BATCH
    MATRIX = DENSE << BATCH_BITS
    assert LANE_USED <= 1 << LANE_BITS and P == 1 << (BATCH_BITS - LANE_BITS)
    BEYOND = 27
    assert MATRIX <= 1 << BEYOND
    LINE = SCATTERED * GROUP // P
    HALO = 40
    LINE_HALO = LINE + 2 * HALO
    MOST = 16.0
    NOWHERE = (1 << 14) - 1
    AHEAD = 3
    PER_CLEAR = 8
    CLEARS = SCATTERED // PER_CLEAR
    PIECES = PER_CLEAR // 2
    assert LANE_USED % (4 * PIECES) == 0
    assert CLEARS * PER_CLEAR == SCATTERED and CLEARS - 1 + AHEAD == DENSE
    STAGE_AT = (8, 3)
    SLACK = STAGE_AT[1] - 1

    with ExitStack() as ctx:
        def sb(name, shape, dt=F32):
            return ctx.enter_context(nc.sbuf_tensor(name, shape, dt))

        def pb(name):
            return ctx.enter_context(nc.psum_tensor(name, [P, 512], F32))

        def sem(name):
            return ctx.enter_context(nc.semaphore(name))

        table_a = nc.dram_tensor("table_a", (BATCHES * BATCH, D), F32).ap()
        table_b = nc.dram_tensor("table_b", (BATCHES * BATCH, D), F32).ap()
        matrix = nc.dram_tensor("matrix", (MATRIX, 1), U8).ap()
        key_dram = nc.dram_tensor("key_dram", (SCATTERED * GROUP,), I32).ap()
        times_dram = nc.dram_tensor("times_dram", (SCATTERED * GROUP,), U8).ap()
        least_dram = nc.dram_tensor("least_dram", (1, GROUPS), F32).ap()
        wide_dram = nc.dram_tensor("wide_dram", (1, GROUPS), F32).ap()
        broken_dram = nc.dram_tensor("broken_dram", (1, P), F32).ap()
        tables = [x, table_a, table_b, table_a, table_b]
        by_lane = matrix.rearrange("(b l c) o -> b l (c o)", l=P, c=1 << LANE_BITS)

        sums_own = sb("sums_own", [P, NODES])
        edge_resid = sb("edge_resid", [P, NODES])
        parts = sb("parts", [P, BLOCKS, PARTS * D], BF16)
        counts = sb("counts", [P, 2, CHUNK, BATCH], FP8)
        near = sb("near", [P, GROUPS, TILES])
        least_all = sb("least_all", [P, GROUPS])
        least_row = sb("least_row", [1, GROUPS], I32)
        wide_row = sb("wide_row", [1, GROUPS], I32)
        uneven_f = sb("uneven_f", [1, 4])
        uneven = sb("uneven", [1, 1], I32)
        index = [sb(f"index{k}", [P, TILES], I32) for k in range(2)]
        times = [sb(f"times{k}", [P, TILES], U8) for k in range(2)]
        gathered = sb("gathered", [P, 2, TILES, D])
        row_parts = sb("row_parts", [P, 2, TILES, PARTS * D], BF16)
        edge_in = sb("edge_in", [P, 2, TILES * ED])
        edge_parts = sb("edge_parts", [P, 2, PARTS, TILES, EXTRA], BF16)
        onehot = sb("onehot", [P, 2, TILES, WINDOW], BF16)
        far = sb("far", [P, 2, TILES])
        far_onehot = sb("far_onehot", [P, TILES, WINDOW], BF16)
        count = sb("count", [P, WINDOW])
        count_far = sb("count_far", [P, WINDOW])
        count_i = sb("count_i", [P, P], I32)
        ident = sb("ident", [P, P])
        center = sb("center", [D, 2 * D])
        mean = sb("mean", [D, 2 * D])
        deg_row = sb("deg_row", [EXTRA, 2 * D])
        weights = sb("weights", [P, LAYERS, 2 * D])
        edge_w = sb("edge_w", [EXTRA, 3, 2 * D])
        bias = sb("bias", [P, 2])
        zeros = sb("zeros", [P, 1])
        shift = sb("shift", [P, 2])
        turned = sb("turned", [TURN, 2, TURNS, D])
        work = sb("work", [P, 4, 2, BATCH])
        r_stage, q_stage, d_stage, dinv = (work[:, n, :, :] for n in range(4))
        table_in = [work[:, n, :, :].rearrange("p k c -> p (k c)").rearrange("p (b d) -> p b d", d=D)
                    for n in range(2)]
        assert CHUNK * D == 2 * BATCH
        h_stage = sb("h_stage", [D, 2, BATCH])
        words = parts[:, :, :].rearrange("p b c -> p (b c)").bitcast(F32)
        by_group = words[0:GROUPS // 2, 0:2 * GROUP].bitcast(I32)
        by_group_f = words[0:GROUPS // 2, 2 * GROUP:4 * GROUP]
        bounds = words[0:GROUPS // 2, 4 * GROUP:4 * GROUP + 6]
        at = 4 * GROUP + 8
        dst_i = words[:, at:at + GROUPS * TILES].bitcast(I32)
        dst_f = words[:, at + GROUPS * TILES:at + 2 * GROUPS * TILES]
        at += 2 * GROUPS * TILES
        ahead = words[:, at:at + LINE // 2].bitcast(BF16)
        behind = words[:, at + LINE // 2:at + LINE].bitcast(BF16)
        place = words[:, at + LINE:at + 2 * LINE].bitcast(I32)
        verdict = words[:, at + 2 * LINE:at + 2 * LINE + 12]
        line_f, batch_f, within_f, pair_f = (words[:, n * LINE_HALO:(n + 1) * LINE_HALO] for n in range(4))
        equal = words[:, 4 * LINE_HALO:4 * LINE_HALO + LINE_HALO // 2].bitcast(BF16)
        assert 9 * LINE_HALO // 2 <= 4 * GROUP and at + 2 * LINE + 12 <= BLOCKS * PARTS * D // 2
        line_words = counts[:, :, :, :].rearrange("p k b c -> p (k b c)").bitcast(I32)
        line_src, line_dst, line_i = (line_words[:, n * LINE_HALO:(n + 1) * LINE_HALO] for n in range(3))
        x_in = work[0:TURN, :, :, :].rearrange("p n k c -> p (n k c)")[:, 0:2 * TURNS * 2 * D]
        x_in = x_in.rearrange("p (k q h d) -> p k q h d", k=2, q=TURNS, h=2)
        row_f = h_stage[0:1, 0, 0:2 * GROUPS].rearrange("o (k g) -> o k g", k=2)
        floor_f = h_stage[0:1, 1, 0:GROUPS]
        ceiling_f = h_stage[0:1, 1, GROUPS:GROUPS + SCATTERED]
        broken_f = h_stage[0:1, 1, GROUPS + SCATTERED:GROUPS + SCATTERED + P]

        window = [pb(f"window{k}") for k in range(2)]
        side = [pb(f"side{k}") for k in range(2)]
        conv = [pb(f"conv{k}") for k in range(2)]
        dense_sum = [pb(f"dense_sum{k}") for k in range(2)]

        names = ("src_in dst_in group_in line_in weights_in const const_i cleared prep least_out least_in "
                 "near_ready index_first onehot_ready summed added group_done split_high split_rest "
                 "split_mid split_low table_high table_rest table_mid table_ready dense_summed "
                 "counts_used dense_added far_onehot far_summed far_added far_prep x_turned x_taken "
                 "deg_ready deg_held conv_ready own_first own_ready cleared_sums result_ready centered "
                 "squared variance var_root dinv_ready new_resid scaled scaled_first turned_ready "
                 "rows_ready row_done rstd_ready sums_done passages uneven_ready floor zeroed "
                 "matrix_cleared keyed keys_out keys_stored pairs verdicts").split()
        S = {n: sem(n) for n in names}
        landed = [sem(f"landed{k}") for k in range(2)]
        fetched = [sem(f"fetched{k}") for k in range(2)]
        scattered = [sem(f"scattered{k}") for k in range(2)]
        edge_landed = [sem(f"edge_landed{k}") for k in range(2)]
        counts_landed = [sem(f"counts_landed{k}") for k in range(2)]
        table_landed = [sem(f"table_landed{k}") for k in range(2)]
        x_landed = [sem(f"x_landed{k}") for k in range(2)]
        stored = [sem(f"stored{k}") for k in range(2)]

        def before(layer, layers=range(LAYERS)):
            return BATCHES * sum(1 for other in layers if other < layer)

        def reach(eng, s, value):
            if not (isinstance(value, int) and value <= 0):
                eng.wait_ge(s, value)

        def reach_alone(eng, s, value):
            if not (isinstance(value, int) and value <= 0):
                eng.wait_ge(s, value)
                if not isinstance(value, int):
                    eng.sem_inc(S["passages"], 1)

        def rounds(eng, body, start, stop):
            with eng.Fori(start, stop) as it:
                body(it)

        def table_loads(layer, c):
            each = [sum(1 for other in range(PER_BATCH) if other % 2 == k) for k in range(2)]
            last = (PER_BATCH - 1) % 2
            extra = 1 if (c % 2 == last and (layer or c == PER_BATCH - 1)) else 0
            return 16 * (layer * each[c % 2] + c // 2 + 1 + extra)

        class Way:
            def __init__(self, uneven):
                self.uneven = uneven
                self.origin = 0 if uneven else SCATTERED
                self.many = GROUPS - self.origin

            def first(self, layer):
                return GROUPS + layer * self.many

        UNEVEN, EVEN = Way(True), Way(False)

        def where(m, kind, k):
            return bass.ds((m * 2 + kind * DENSE + k) * BATCH, BATCH)

        def spots(m, kind):
            return [(k, m * 4 + kind * 2 + k, where(m, kind, k)) for k in range(2)]

        def propagate(eng, group, stages, behind=None):
            def round_of(r):
                for p in range(PER_ROUND):
                    group(OPENING + r * PER_ROUND + p, p % 2, r, p)
                    if p - STAGE_AT[1] in stages and not (isinstance(r, int) and r == 0):
                        stages[p - STAGE_AT[1]](r - 1, 1)
                    if p - STAGE_AT[0] in stages:
                        stages[p - STAGE_AT[0]](r, 0)
                    if behind:
                        behind(r, p)

            for k in range(OPENING):
                group(k, k, None, None)
            round_of(0)
            rounds(eng, round_of, 1, ROUNDS - 1)
            round_of(ROUNDS - 1)

        def finish(stages):
            for step in sorted(stages):
                stages[step](ROUNDS - 1, 1)

        def chunk_number(layer, r, p):
            if r is None:
                return layer * ROUNDS * PER_ROUND + p
            return r * PER_ROUND + (layer * ROUNDS * PER_ROUND + PER_BATCH + p)

        def chunk_slot(r, p):
            return (p if r is None else p + PER_BATCH) % 2

        def chunk_landings(layer, r, p):
            if r is None or isinstance(r, int):
                return chunk_number(layer, r, p) // 2
            return r * (PER_ROUND // 2) + chunk_number(layer, 0, p) // 2

        def has_chunk(r, p):
            return r is None or not isinstance(r, int) or r < ROUNDS - 1 or p < PER_BATCH

        def whole_phase(eng, stages):
            def step_of(m):
                for kind in range(2):
                    for step in sorted(stages):
                        stages[step](m, kind)

            step_of(0)
            rounds(eng, step_of, 1, ROUNDS)

        def all_pairs(eng, group, start, stop):
            def pair_of(pair):
                for k in range(2):
                    group(pair * 2 + k, k)
            if start == 0:
                pair_of(0)
            rounds(eng, pair_of, max(start, 1), stop)

        TABLE_BEFORE = {0: (0, 1), 1: (2, 3), 2: (4, 5, 6)}
        assert sorted(sum(TABLE_BEFORE.values(), ())) == list(range(PER_BATCH))

        block = ctx.enter_context(nc.Block())

        @block.sync
        def _(sp):
            full, tail = FULL * GROUP, TAIL
            pairs = GROUPS // 2
            sp.wait_ge(S["cleared"], 5)
            sp.dma_start(by_group[0:pairs - 1, :],
                         dst[0:(pairs - 1) * 2 * GROUP].rearrange("(p e) -> p e", p=pairs - 1)).then_inc(S["group_in"], 16)
            sp.dma_start(by_group[pairs - 1:pairs, 0:E - (pairs - 1) * 2 * GROUP],
                         dst[(pairs - 1) * 2 * GROUP:E].rearrange("(p e) -> p e", p=1)).then_inc(S["group_in"], 16)
            for host, held in ((src, line_src), (dst, line_dst)):
                edges = SCATTERED * GROUP
                sp.dma_start(held[:, HALO:HALO + LINE], host[0:edges].rearrange("(p c) -> p c", p=P)
                             ).then_inc(S["line_in"], 16)
                sp.dma_start(held[1:P, 0:HALO], host[0:edges].rearrange("(p c) -> p c", p=P)[0:P - 1, LINE - HALO:LINE]
                             ).then_inc(S["line_in"], 16)
                sp.dma_start(held[0:P - 1, HALO + LINE:LINE_HALO],
                             host[0:edges].rearrange("(p c) -> p c", p=P)[1:P, 0:HALO]).then_inc(S["line_in"], 16)
            sp.dma_start(line_dst[P - 1:P, HALO + LINE:LINE_HALO],
                         dst[edges:edges + HALO].rearrange("(o c) -> o c", o=1)).then_inc(S["line_in"], 16)
            sp.dma_start(dst_i[:, 0:FULL * TILES].rearrange("p (g j) -> p g j", j=TILES),
                         dst[0:full].rearrange("(g p j) -> p g j", p=P, j=TILES)).then_inc(S["dst_in"], 16)
            sp.dma_start(dst_i[0:tail, FULL * TILES:GROUPS * TILES],
                         dst[full:E].rearrange("(p j) -> p j", j=TILES)).then_inc(S["dst_in"], 16)

            def clear_matrix(batch, piece):
                size = LANE_USED // PIECES
                sp.dma_start(by_lane[bass.ds(batch, 1), :, piece * size:(piece + 1) * size].rearrange("o l c -> l (o c)"),
                             sums_own[:, 0:size // 4].bitcast(U8)).then_inc(S["matrix_cleared"], 16)

            def take_x(pair):
                for k in range(2):
                    batch = pair * 2 + k
                    held = min(BATCH, N - batch * BATCH) if isinstance(pair, int) else BATCH
                    reach_alone(sp, S["x_turned"], batch - 1)
                    whole, rest = divmod(held, TURN)
                    for half in range(2):
                        of = x[bass.ds(batch * BATCH, whole * TURN), :].rearrange("(q p) d -> p q d", p=TURN)
                        sp.dma_start(x_in[:, k, 0:whole, half, :], of).then_inc(x_landed[k], 16)
                        if rest:
                            sp.dma_start(x_in[0:rest, k, whole, half, :], x[N - rest:N, :]).then_inc(x_landed[k], 16)

            sp.wait_ge(S["prep"], 7)
            sp.dma_start(least_dram.rearrange("o (p k) -> (o p) k", k=2), bounds[:, 0:2]).then_inc(S["least_out"], 16)
            sp.dma_start(wide_dram.rearrange("o (p k) -> (o p) k", k=2), bounds[:, 4:6]).then_inc(S["least_out"], 16)
            sp.wait_ge(S["least_out"], 32)
            sp.dma_start(least_all[:, :], least_dram.to_broadcast((P, GROUPS))).then_inc(S["least_in"], 16)
            sp.dma_start(row_f[:, 0, :], least_dram).then_inc(S["least_in"], 16)
            sp.dma_start(row_f[:, 1, :], wide_dram).then_inc(S["least_in"], 16)
            take_x(0)
            rounds(sp, take_x, 1, BATCHES // 2 - 1)
            take_x(BATCHES // 2 - 1)
            sp.wait_ge(S["zeroed"], 1)
            for batch in range(AHEAD):
                for piece in range(PIECES):
                    clear_matrix(batch, piece)

            n = 0
            for layer in range(LAYERS):
                for half in range(2):
                    c = slice(half * D, (half + 1) * D)
                    if layer < GCN1:
                        loads = ((weights[0:D, layer, c], W[layer][D:2 * D, :]),
                                 (weights[D:2 * D, layer, c], W[layer][0:D, :]),
                                 (edge_w[0:ED, layer, c], W[layer][2 * D:2 * D + ED, :]),
                                 (edge_w[ED:EXTRA, layer, c], b[layer].rearrange("(o d) -> o d", o=1)))
                    else:
                        loads = ((weights[0:D, layer, c], W[layer]), (weights[D:2 * D, layer, c], W[layer]),
                                 (bias[half * D:half * D + D, layer - GCN1:layer - GCN1 + 1],
                                  b[layer].rearrange("(d o) -> d o", o=1)))
                    for to, of in loads:
                        sp.dma_start(to, of).then_inc(S["weights_in"], 16)
                        n += 1
            assert n == WEIGHT_LOADS

            sp.wait_ge(S["keyed"], 1)
            sp.dma_start(key_dram.rearrange("(p c) -> p c", p=P), place).then_inc(S["keys_out"], 16)
            sp.dma_start(times_dram.rearrange("(p c) -> p c", p=P),
                         line_i.bitcast(U8)[:, 0:LINE]).then_inc(S["keys_out"], 16)
            sp.dma_start(broken_dram.rearrange("o p -> p o"), verdict[:, 8:9]).then_inc(S["keys_out"], 16)
            sp.wait_ge(S["keys_out"], 48)
            sp.dma_start(broken_f, broken_dram).then_inc(S["keys_stored"], 16)

            def attributes(g, k):
                held = TAIL if isinstance(g, int) and g == FULL else P
                reach_alone(sp, S["split_low"], g - 1)
                sp.dma_start(edge_in[0:held, k, :],
                             edge_attr[bass.ds(g * GROUP, held * TILES), :].rearrange("(p j) d -> p (j d)", j=TILES)
                             ).then_inc(edge_landed[k], 16)

            def both_attributes(pair):
                for k in range(2):
                    attributes(pair * 2 + k, k)

            def keys(pair, k):
                span = bass.ds((pair * 2 + k) * GROUP, GROUP)
                reach_alone(sp, scattered[k], pair * TILES * 16)
                sp.dma_start(index[k][:, :], key_dram[span].rearrange("(p j) -> p j", p=P)).then_inc(fetched[k], 16)
                sp.dma_start(times[k][:, :], times_dram[span].rearrange("(p j) -> p j", p=P)).then_inc(fetched[k], 16)

            def sources(way, layer, g, k):
                held = TAIL if isinstance(g, int) and way.origin + g == FULL else P
                gathers = (layer * way.many + g) // 2 if isinstance(g, int) else None
                if gathers is None:
                    gathers = layer * (way.many // 2) + (g - k) // 2
                reach_alone(sp, landed[k], gathers * TILES * 16)
                of = src[bass.ds((way.origin + g) * GROUP, held * TILES)]
                sp.dma_start(index[k][0:held, :], of.rearrange("(p j) -> p j", j=TILES)).then_inc(fetched[k], 16)

            def store(layer, m, kind):
                for k, n, nodes in spots(m, kind):
                    reach_alone(sp, S["rows_ready"], before(layer) + n + 1)
                    batch = m * 2 + kind * DENSE + k
                    to = tables[layer + 1] if layer < LAYERS - 1 else out
                    if layer < LAYERS - 1 or not isinstance(m, int) or (batch + 1) * BATCH <= N:
                        sp.dma_start(to[nodes, :].rearrange("(q p) d -> p q d", p=TURN),
                                     turned[:, k, :, :]).then_inc(stored[k], 16)
                    else:
                        first = batch * BATCH
                        whole = (N - first) // TURN
                        rest = N - first - whole * TURN
                        sp.dma_start(out[first:first + whole * TURN, :].rearrange("(q p) d -> p q d", p=TURN),
                                     turned[:, k, 0:whole, :]).then_inc(stored[k], 16)
                        sp.dma_start(out[N - rest:N, :], turned[0:rest, k, whole, :]).then_inc(stored[k], 16)

            def table_load(layer):
                if layer:
                    sp.wait_ge(stored[0], 8 * BATCHES * layer)
                    sp.wait_ge(stored[1], 8 * BATCHES * layer)
                    sp.wait_ge(S["own_ready"], before(layer))
                for c in range(PER_BATCH):
                    reach_alone(sp, S["table_ready"], layer * PER_BATCH + c - 1)
                    first, last = c * CHUNK * P, min((c + 1) * CHUNK * P, tables[layer].shape[0])
                    whole, rest = divmod(last - first, P)
                    sp.dma_start(table_in[c % 2][:, 0:whole, :],
                                 tables[layer][first:first + whole * P, :].rearrange("(b l) d -> l b d", l=P)
                                 ).then_inc(table_landed[c % 2], 16)
                    if rest:
                        sp.dma_start(table_in[c % 2][0:rest, whole, :], tables[layer][last - rest:last, :]
                                     ).then_inc(table_landed[c % 2], 16)
                    matrix_chunk(layer, None, c)

            def matrix_chunk(layer, r, p):
                batch, c = divmod(p, PER_BATCH)
                if r is not None:
                    batch = r * 2 + (batch + 1)
                slot = chunk_slot(r, p)
                reach_alone(sp, S["counts_used"], chunk_number(layer, r, p) - 1)
                of = by_lane[bass.ds(batch, 1), :, c * CHUNK * BATCH:(c + 1) * CHUNK * BATCH]
                sp.dma_start(counts[:, slot, :, :].bitcast(U8).rearrange("p b c -> p (b c)"),
                             of.rearrange("o l c -> l (o c)")).then_inc(counts_landed[slot], 16)

            sp.wait_ge(S["uneven_ready"], 1)
            is_uneven = sp.value_load(uneven[0:1, 0:1], min_val=0, max_val=1)
            with sp.If(is_uneven > 0):
                both_attributes(0)
                rounds(sp, both_attributes, 1, GROUPS // 2 - 1)
                both_attributes(GROUPS // 2 - 1)
                for layer in range(LAYERS):
                    way = UNEVEN
                    for g in range(2):
                        sources(way, layer, g, g)
                    rounds(sp, lambda pair: [sources(way, layer, pair * 2 + k, k) for k in range(2)], 1, GROUPS // 2 - 1)
                    for g in range(GROUPS - 2, GROUPS):
                        sources(way, layer, g, g % 2)

                    def stores(m):
                        for kind in range(2):
                            store(layer, m, kind)

                    rounds(sp, stores, 0, ROUNDS - 1)
                    stores(ROUNDS - 1)
            with sp.If(is_uneven < 1):
                def clearing(q):
                    for s in range(PIECES):
                        pair = q * PIECES + s
                        for k in range(2):
                            keys(pair, k)
                            both_attributes(pair * 2 + k)
                        if not isinstance(q, int) or q + AHEAD < DENSE:
                            clear_matrix(q + AHEAD, s)

                clearing(0)
                rounds(sp, clearing, 1, CLEARS - 1)
                clearing(CLEARS - 1)
                for pair in range(SCATTERED, GROUPS // 2):
                    both_attributes(pair)
                for k in range(2):
                    sp.wait_ge(scattered[k], SCATTERED // 2 * TILES * 16)
                for layer in range(LAYERS):
                    for g in range(OPENING):
                        sources(EVEN, layer, g, g)
                    table_load(layer)

                    def round_of(r):
                        for p in range(PER_ROUND):
                            if has_chunk(r, p):
                                matrix_chunk(layer, r, p)
                            if p == STAGE_AT[1] + 5 and not (isinstance(r, int) and r == 0):
                                store(layer, r - 1, 1)
                            if p == STAGE_AT[0] + 5:
                                store(layer, r, 0)

                    round_of(0)
                    rounds(sp, round_of, 1, ROUNDS - 1)
                    round_of(ROUNDS - 1)
                    store(layer, ROUNDS - 1, 1)
            sp.wait_ge(stored[0], 8 * LAYERS * BATCHES)
            sp.wait_ge(stored[1], 8 * LAYERS * BATCHES + 16)

        @block.gpsimd
        def _(pool):
            pool.iota(count_i[:, :], pattern=[[1, P]], base=0, channel_multiplier=0).then_inc(S["const_i"], 1)
            pool.wait_ge(S["const"], 2)
            pool.iota(count_i[:, :], pattern=[[1, P]], base=0, channel_multiplier=-1).then_inc(S["const_i"], 1)
            pool.wait_ge(S["const"], 3)
            pool.iota(count_i[0:D, :], pattern=[[0, 2], [1, D]], base=0, channel_multiplier=-1).then_inc(S["const_i"], 1)
            pool.wait_ge(S["const"], 4)
            pool.iota(count_i[0:EXTRA, :], pattern=[[0, P]], base=0, channel_multiplier=1).then_inc(S["const_i"], 1)

            def scatter(pair):
                for k in range(2):
                    reach_alone(pool, fetched[k], pair * 32 + 32)
                    for j in range(TILES):
                        pool.indirect_dma_start(
                            out=matrix, out_offset=bass.IndirectOffsetOnAxis(ap=index[k][:, j:j + 1], axis=0),
                            in_=times[k][:, j:j + 1], in_offset=None,
                            bounds_check=MATRIX - 1, oob_is_err=False).then_inc(scattered[k], 16)

            def gather(way, layer, g, k, base):
                if isinstance(g, int):
                    gathers = (layer * way.many + g) // 2
                else:
                    gathers = layer * (way.many // 2) + (g - k) // 2
                reach_alone(pool, fetched[k], base + gathers * 16 + 16)
                reach_alone(pool, S["split_low"], way.first(layer) + g - 1)
                for j in range(TILES):
                    pool.indirect_dma_start(
                        out=gathered[:, k, j, :], out_offset=None, in_=tables[layer],
                        in_offset=bass.IndirectOffsetOnAxis(ap=index[k][:, j:j + 1], axis=0),
                    ).then_inc(landed[k], 16)

            def table_written(layer):
                if layer:
                    for k in range(2):
                        pool.wait_ge(stored[k], 8 * layer * BATCHES)

            pool.wait_ge(S["uneven_ready"], 1)
            is_uneven = pool.value_load(uneven[0:1, 0:1], min_val=0, max_val=1)
            with pool.If(is_uneven > 0):
                for layer in range(LAYERS):
                    table_written(layer)
                    all_pairs(pool, lambda g, k: gather(UNEVEN, layer, g, k, 0), 0, GROUPS // 2)
            with pool.If(is_uneven < 1):
                def clearing(q):
                    reach_alone(pool, S["matrix_cleared"], q * (16 * PIECES) + AHEAD * 16 * PIECES)
                    for s in range(PER_CLEAR // 2):
                        scatter(q * (PER_CLEAR // 2) + s)

                rounds(pool, clearing, 0, CLEARS)
                base = SCATTERED // 2 * 32
                for layer in range(LAYERS):
                    table_written(layer)
                    all_pairs(pool, lambda g, k: gather(EVEN, layer, g, k, base), 0, LOOSE // 2)

        @block.scalar
        def _(act):
            def split_edges(spent, g, k):
                rows = edge_in[:, k, :].rearrange("p (j d) -> p j d", d=ED)
                reach(act, edge_landed[k], (g - k) // 2 * 16 + 16)
                reach(act, spent, g - 1)
                act.copy(edge_parts[:, k, 0, :, 0:ED], rows).then_inc(S["split_high"], 1)
                reach(act, S["split_rest"], g + 1)
                act.copy(edge_parts[:, k, 1, :, 0:ED], rows).then_inc(S["split_mid"], 1)

            def split_rows(way, layer, spent, g, k):
                u = way.first(layer) + g
                if isinstance(g, int):
                    gathers = (layer * way.many + g) // 2
                else:
                    gathers = layer * (way.many // 2) + (g - k) // 2
                reach_alone(act, landed[k], gathers * TILES * 16 + TILES * 16)
                if not way.uneven and not (isinstance(g, int) and g + 2 >= way.many):
                    held = TAIL if isinstance(g, int) and way.origin + g + 2 == FULL else P
                    of = src[bass.ds((way.origin + g + 2) * GROUP, held * TILES)]
                    act.dma_start(index[k][0:held, :], of.rearrange("(p j) -> p j", j=TILES)).then_inc(fetched[k], 16)
                reach(act, spent, u - 1)
                act.copy(row_parts[:, k, :, 0:D], gathered[:, k, :, :]).then_inc(S["split_high"], 1)
                reach(act, S["split_rest"], u + 1)
                act.copy(row_parts[:, k, :, D:2 * D], gathered[:, k, :, :]).then_inc(S["split_mid"], 1)

            def split_table(layer, g):
                for c in TABLE_BEFORE.get(g, ()) if isinstance(g, int) else ():
                    n = layer * PER_BATCH + c
                    blocks = slice(c * CHUNK, (c + 1) * CHUNK)
                    act.wait_ge(table_landed[c % 2], table_loads(layer, c))
                    act.copy(parts[:, blocks, 0:D], table_in[c % 2]).then_inc(S["table_high"], 1)
                    act.wait_ge(S["table_rest"], n + 1)
                    act.copy(parts[:, blocks, D:2 * D], table_in[c % 2]).then_inc(S["table_mid"], 1)

            def stages(layer):
                ln = before(layer, (LN1, LN2))
                sq = before(layer, (LN1, GCN1, LN2))

                def hold_degree(m, kind):
                    for k, n, nodes in spots(m, kind):
                        reach(act, S["deg_ready"], before(layer) + n + 1)
                        reach(act, S["own_ready"], before(layer) + n - 1)
                        act.copy(d_stage[:, k, :], side[k][:, 0:BATCH]).then_inc(S["deg_held"], 1)

                def degree_root(m, kind):
                    for k, n, nodes in spots(m, kind):
                        reach(act, S["result_ready"], before(layer) + n - 1)
                        reach(act, S["deg_ready"], before(layer) + n + 1)
                        act.activation(d_stage[:, k, :], side[k][:, 0:BATCH], ACT.Sqrt,
                                       bias=shift[:, 0:1]).then_inc(S["deg_held"], 1)

                def clear_sums(m, kind):
                    for k, n, nodes in spots(m, kind):
                        reach_alone(act, S["conv_ready"], before(layer) + n + 1)
                        act.copy(sums_own[0:D, nodes], zeros[0:D, :].to_broadcast((D, BATCH))
                                 ).then_inc(S["cleared_sums"], 1)

                def relu(m, kind):
                    for k, n, nodes in spots(m, kind):
                        reach(act, S["conv_ready"], before(layer) + n + 1)
                        reach(act, S["turned_ready"], before(layer) + n - 1)
                        act.activation(h_stage[:, k, :], conv[k][0:D, 0:BATCH], ACT.Relu).then_inc(S["result_ready"], 1)
                    clear_sums(m, kind)

                def square(m, kind):
                    for k, n, nodes in spots(m, kind):
                        reach(act, S["centered"], ln + n + 1)
                        reach(act, S["rstd_ready"], ln + n - 1)
                        act.activation(q_stage[0:D, k, :], conv[k][0:D, 0:BATCH],
                                       ACT.Square).then_inc(S["squared"], 1)

                def deviation(m, kind):
                    for k, n, nodes in spots(m, kind):
                        reach(act, S["variance"], ln + n + 1)
                        act.activation(q_stage[:, k, :], side[k][:, 0:BATCH], ACT.Sqrt,
                                       bias=shift[:, 1:2]).then_inc(S["var_root"], 1)

                def gcn_relu(m, kind):
                    for k, n, nodes in spots(m, kind):
                        reach(act, S["scaled"], sq + n + 1)
                        reach(act, S["result_ready"], before(layer) + n - 1)
                        reach(act, S["own_ready"], before(layer) + n - 1)
                        act.activation(q_stage[:, k, :], r_stage[:, k, :], ACT.Relu,
                                       bias=bias[:, 0:1]).then_inc(S["squared"], 1)

                def rows(m, kind):
                    for k, n, nodes in spots(m, kind):
                        reach(act, S["turned_ready"], before(layer) + n + 1)
                        reach(act, stored[k], m * 32 + (kind * 16 + layer * 8 * BATCHES))
                        act.copy(turned[:, k, :, :].rearrange("p q d -> p (q d)"),
                                 side[k][0:TURN, 0:TURNS * D]).then_inc(S["rows_ready"], 1)

                def square_and_root(m, kind):
                    square(m, kind)
                    degree_root(m, kind)

                return {0: {0: hold_degree, 2: relu, 4: rows},
                        1: {0: hold_degree, 1: relu, 3: rows},
                        LN1: {1: clear_sums, 2: square_and_root, 3: deviation, 5: rows},
                        GCN1: {0: degree_root, 1: clear_sums, 2: gcn_relu, 4: rows},
                        LN2: {0: degree_root, 2: square, 3: deviation, 5: rows}}[layer]

            act.wait_ge(S["const"], 1)
            act.copy(sums_own[:, :], zeros[:, :].to_broadcast((P, NODES))).then_inc(S["zeroed"], 1)
            act.copy(edge_resid[0:EXTRA, :], zeros[0:EXTRA, :].to_broadcast((EXTRA, NODES))).then_inc(S["zeroed"], 1)

            def take_x(pair):
                for k in range(2):
                    batch = pair * 2 + k
                    reach_alone(act, S["x_turned"], batch + 1)
                    act.copy(edge_resid[D:2 * D, bass.ds(batch * BATCH, BATCH)],
                             conv[k][D:2 * D, 0:BATCH]).then_inc(S["x_taken"], 1)

            take_x(0)
            rounds(act, take_x, 1, BATCHES // 2)
            act.wait_ge(S["const"], 11)
            act.wait_ge(S["uneven_ready"], 1)
            act.wait_ge(S["weights_in"], 16 * WEIGHT_LOADS)
            is_uneven = act.value_load(uneven[0:1, 0:1], min_val=0, max_val=1)
            with act.If(is_uneven > 0):
                all_pairs(act, lambda g, k: split_edges(S["group_done"], g, k), 0, GROUPS // 2)
                for layer in range(LAYERS):
                    all_pairs(act, lambda g, k: split_rows(UNEVEN, layer, S["group_done"], g, k), 0, GROUPS // 2)
                    whole_phase(act, stages(layer))
            with act.If(is_uneven < 1):
                all_pairs(act, lambda g, k: split_edges(S["summed"], g, k), 0, GROUPS // 2)
                for layer in range(LAYERS):
                    def group(g, k, r, p):
                        split_table(layer, g)
                        split_rows(EVEN, layer, S["summed"], g, k)

                    propagate(act, group, stages(layer))
                    finish(stages(layer))

        @block.vector
        def _(dve):
            dve.memset(by_group[96:GROUPS // 2, :], -1).then_inc(S["cleared"], 1)
            dve.memset(line_src[:, 0:HALO], NOWHERE).then_inc(S["cleared"], 1)
            dve.memset(line_src[:, HALO + LINE:LINE_HALO], NOWHERE).then_inc(S["cleared"], 1)
            dve.memset(line_dst[:, 0:HALO], 0).then_inc(S["cleared"], 1)
            dve.memset(dst_i[:, FULL * TILES:GROUPS * TILES], -1).then_inc(S["cleared"], 1)
            dve.memset(zeros[:, :], 0.0).then_inc(S["const"], 1)
            dve.wait_ge(S["const_i"], 1)
            dve.tensor_copy(count[:, :], count_i[:, 0:WINDOW]).then_inc(S["const"], 1)
            dve.wait_ge(S["const_i"], 2)
            dve.tensor_scalar(ident[:, :], count_i[:, :], 0.0, None, ALU.is_equal).then_inc(S["const"], 1)
            dve.wait_ge(S["const_i"], 3)
            dve.tensor_scalar(center[:, :], count_i[0:D, :], 0.0, -1.0 / D, ALU.is_equal, ALU.add).then_inc(S["const"], 1)
            dve.wait_ge(S["const_i"], 4)
            dve.tensor_scalar(deg_row[:, :], count_i[0:EXTRA, :], float(ED), None, ALU.is_equal).then_inc(S["const"], 1)
            dve.memset(mean[:, :], 1.0 / D).then_inc(S["const"], 1)
            dve.memset(shift[:, 0:1], 1.0).then_inc(S["const"], 1)
            dve.memset(shift[:, 1:2], EPS).then_inc(S["const"], 1)
            for part in range(PARTS):
                dve.memset(edge_parts[:, :, part, :, ED:EXTRA], 0.0 if part else 1.0).then_inc(S["const"], 1)

            pair = "p (k e) -> p k e"
            dve.wait_ge(S["group_in"], 32)
            dve.tensor_copy(by_group_f, by_group).then_inc(S["prep"], 1)
            dve.wait_ge(S["prep"], 1)
            dve.tensor_reduce(bounds[:, 2:4], by_group_f.rearrange(pair, k=2), AX.X, ALU.max).then_inc(S["prep"], 1)
            held = by_group.bitcast(F32)
            dve.tensor_scalar(held, by_group_f, 0.0, float(N), ALU.is_lt, ALU.mult).then_inc(S["prep"], 1)
            dve.wait_ge(S["prep"], 3)
            dve.tensor_tensor(held, held, by_group_f, ALU.add).then_inc(S["prep"], 1)
            dve.wait_ge(S["prep"], 4)
            dve.tensor_reduce(bounds[:, 0:2], held.rearrange(pair, k=2), AX.X, ALU.min).then_inc(S["prep"], 1)
            dve.wait_ge(S["prep"], 5)
            dve.tensor_tensor(bounds[:, 2:4], bounds[:, 2:4], bounds[:, 0:2], ALU.subtract).then_inc(S["prep"], 1)
            dve.wait_ge(S["prep"], 6)
            dve.tensor_scalar(bounds[:, 4:6], bounds[:, 2:4], float(WINDOW), None, ALU.is_ge).then_inc(S["prep"], 1)

            steps = [0]

            def then(ins):
                ins.then_inc(S["pairs"], 1)
                steps[0] += 1
                dve.wait_ge(S["pairs"], steps[0])

            dve.wait_ge(S["line_in"], 16 * 7)
            then(dve.tensor_copy(line_f, line_dst))
            then(dve.tensor_scalar(line_i, line_f, 1.0 / BATCH, None, ALU.mult))
            then(dve.tensor_copy(batch_f, line_i))
            then(dve.scalar_tensor_tensor(out=within_f, in0=batch_f, scalar=-float(BATCH), in1=line_f,
                                          op0=ALU.mult, op1=ALU.add))
            then(dve.tensor_scalar(pair_f, within_f, 0.0, None, ALU.is_lt))
            then(dve.tensor_tensor(batch_f, batch_f, pair_f, ALU.subtract))
            then(dve.scalar_tensor_tensor(out=within_f, in0=pair_f, scalar=float(BATCH), in1=within_f,
                                          op0=ALU.mult, op1=ALU.add))
            then(dve.tensor_copy(pair_f, line_src))
            then(dve.scalar_tensor_tensor(out=pair_f, in0=within_f, scalar=float(NOWHERE + 1), in1=pair_f,
                                          op0=ALU.mult, op1=ALU.add))
            own = slice(HALO, HALO + LINE)
            lane, blk = line_src[:, own], line_dst[:, own]
            one = slice(HALO + 1, HALO + LINE + 1)
            off = slice(2 * HALO, LINE_HALO)
            then(dve.tensor_tensor(place.bitcast(F32), line_f[:, one], line_f[:, own], ALU.subtract))
            then(dve.tensor_reduce(verdict[:, 0:1], place.bitcast(F32), AX.X, ALU.min))
            then(dve.tensor_tensor(place.bitcast(F32), line_f[:, off], line_f[:, own], ALU.subtract))
            then(dve.tensor_reduce(verdict[:, 1:2], place.bitcast(F32), AX.X, ALU.min))
            then(dve.tensor_reduce(verdict[:, 2:3], place.bitcast(F32), AX.X, ALU.max))
            then(dve.tensor_reduce(verdict[:, 3:4], line_f[:, own], AX.X, ALU.max))
            then(dve.tensor_scalar(verdict[:, 4:5], verdict[:, 0:1], 0.0, None, ALU.is_lt))
            then(dve.tensor_scalar(verdict[:, 5:6], verdict[:, 1:2], 1.0, None, ALU.is_lt))
            then(dve.tensor_scalar(verdict[:, 6:7], verdict[:, 2:3], float(BATCH), None, ALU.is_ge))
            then(dve.tensor_scalar(verdict[:, 7:8], verdict[:, 3:4], float(DENSE * BATCH), None, ALU.is_ge))
            then(dve.tensor_scalar(line_i[:, own], line_src[:, own], P.bit_length() - 1, None,
                                   ALU.logical_shift_right))
            then(dve.tensor_copy(place.bitcast(F32), line_i[:, own]))
            then(dve.scalar_tensor_tensor(out=within_f[:, own], in0=place.bitcast(F32), scalar=float(BATCH),
                                          in1=within_f[:, own], op0=ALU.mult, op1=ALU.add))
            then(dve.tensor_scalar(lane, lane, P - 1, LANE_BITS, ALU.bitwise_and, ALU.logical_shift_left))
            then(dve.tensor_copy(place, within_f[:, own]))
            then(dve.tensor_tensor(place, place, lane, ALU.bitwise_or))
            then(dve.tensor_copy(blk, batch_f[:, own]))
            then(dve.tensor_scalar(blk, blk, BATCH_BITS, None, ALU.logical_shift_left))
            then(dve.tensor_tensor(place, place, blk, ALU.bitwise_or))
            then(dve.memset(ahead, 0.0))
            then(dve.memset(behind, 0.0))
            wide = HALO + LINE
            dve.sem_inc(S["verdicts"], 3)
            with dve.Fori(1, HALO) as d:
                dve.wait_ge(S["verdicts"], d * 3)
                dve.tensor_tensor(equal[:, 0:wide], pair_f[:, 0:wide], pair_f[:, bass.ds(d, wide)],
                                  ALU.is_equal).then_inc(S["verdicts"], 1)
                dve.wait_ge(S["verdicts"], d * 3 + 1)
                dve.tensor_tensor(ahead, ahead, equal[:, HALO:wide], ALU.add).then_inc(S["verdicts"], 1)
                dve.tensor_tensor(behind, behind, equal[:, bass.ds(HALO - d, LINE)], ALU.add).then_inc(S["verdicts"], 1)
            dve.wait_ge(S["verdicts"], HALO * 3)
            then(dve.tensor_scalar(blk, ahead, 1.0, None, ALU.is_ge))
            then(dve.tensor_scalar(blk, blk, BEYOND, None, ALU.logical_shift_left))
            then(dve.tensor_tensor(place, place, blk, ALU.bitwise_or))
            then(dve.tensor_scalar(within_f[:, own], behind, 1.0, None, ALU.add))
            then(dve.tensor_copy(line_i.bitcast(FP8)[:, 0:LINE], within_f[:, own], saturate=False))
            then(dve.tensor_reduce(verdict[:, 3:4], within_f[:, own], AX.X, ALU.max))
            then(dve.tensor_scalar(verdict[:, 3:4], verdict[:, 3:4], MOST, None, ALU.is_gt))
            then(dve.tensor_reduce(verdict[:, 8:9], verdict[:, 3:8], AX.X, ALU.max))
            dve.sem_inc(S["keyed"], 1)

            dve.wait_ge(S["dst_in"], 32)
            dve.tensor_copy(dst_f, dst_i).then_inc(S["near_ready"], 1)
            dve.wait_ge(S["near_ready"], 1)
            dve.wait_ge(S["least_in"], 48)
            dve.tensor_tensor(near[:, :, :], dst_f.rearrange("p (g j) -> p g j", j=TILES),
                              least_all[:, :].unsqueeze(2).to_broadcast((P, GROUPS, TILES)),
                              ALU.subtract).then_inc(S["near_ready"], 1)
            dve.tensor_copy(least_row[:, :], row_f[:, 0, :]).then_inc(S["row_done"], 1)
            dve.tensor_copy(wide_row[:, :], row_f[:, 1, :]).then_inc(S["row_done"], 1)
            floors = [(0, 0), (SCATTERED, (DENSE - 2) * BATCH)]
            floors += [(SCATTERED + OPENING + PER_ROUND * (m + 1) + SLACK, (DENSE + 2 * m + 2) * BATCH)
                       for m in range(ROUNDS - 1)]
            for (first, nodes), (last, _) in zip(floors, floors[1:] + [(GROUPS, 0)]):
                dve.memset(floor_f[:, first:last], float(nodes)).then_inc(S["floor"], 1)
            for q in range(CLEARS):
                dve.memset(ceiling_f[:, q * PER_CLEAR:(q + 1) * PER_CLEAR],
                           float((q + AHEAD) * BATCH)).then_inc(S["floor"], 1)
            checks = len(floors) + CLEARS
            dve.wait_ge(S["floor"], checks)
            dve.tensor_tensor(floor_f, row_f[:, 0, :], floor_f, ALU.is_lt).then_inc(S["floor"], 1)
            dve.tensor_tensor(ceiling_f, row_f[:, 0, 1:SCATTERED + 1], ceiling_f, ALU.is_ge).then_inc(S["floor"], 1)
            dve.tensor_reduce(uneven_f[:, 1:2], row_f[:, 1, :], AX.X, ALU.max).then_inc(S["floor"], 1)
            dve.wait_ge(S["floor"], checks + 3)
            dve.tensor_reduce(uneven_f[:, 0:1], floor_f, AX.X, ALU.max).then_inc(S["floor"], 1)
            dve.tensor_reduce(uneven_f[:, 2:3], ceiling_f, AX.X, ALU.max).then_inc(S["floor"], 1)
            dve.wait_ge(S["keys_stored"], 16)
            dve.tensor_reduce(uneven_f[:, 3:4], broken_f, AX.X, ALU.max).then_inc(S["floor"], 1)
            dve.wait_ge(S["floor"], checks + 6)
            dve.tensor_reduce(uneven[:, :], uneven_f[:, :], AX.X, ALU.max).then_inc(S["uneven_ready"], 1)
            dve.wait_ge(S["near_ready"], 2)
            dve.wait_ge(S["row_done"], 2)

            dve.wait_ge(S["uneven_ready"], 1)

            def of_group(targets, g):
                return targets[:, bass.ds(g, 1), :].rearrange("p o j -> p (o j)")

            def spread(targets):
                return targets.unsqueeze(2).to_broadcast((P, TILES, WINDOW))

            def each(row):
                return row.unsqueeze(1).to_broadcast((P, TILES, WINDOW))

            def add_at(layer, bank, at, done):
                to = edge_resid[0:EXTRA, bass.ds(at, WINDOW)] if layer is None else sums_own[0:D, bass.ds(at, WINDOW)]
                held = EXTRA if layer is None else D
                dve.tensor_tensor(to, bank[0:held, 0:WINDOW], to, ALU.add).then_inc(done, 1)

            def add(layer, first, origin, g, k):
                reach(dve, S["summed"], first + g + 1)
                reach(dve, S["added"], first + g)
                at = dve.value_load(least_row[0:1, bass.ds(origin + g, 1)], min_val=0, max_val=N - 1)
                add_at(layer, window[k], at, S["added"])

            def add_far(layer, first, g):
                wide = dve.value_load(wide_row[0:1, bass.ds(g, 1)], min_val=0, max_val=1)
                with dve.If(wide > 0):
                    reach(dve, S["added"], first + g + 1)
                    dve.tensor_scalar(far[:, 0, :], of_group(near, g), least_all[:, bass.ds(g, 1)], 1.0,
                                      ALU.add, ALU.add).then_inc(S["far_prep"], 1)
                    dve.tensor_scalar(far[:, 1, :], of_group(near, g), float(WINDOW), None,
                                      ALU.is_ge).then_inc(S["far_prep"], 1)
                    dve.tensor_scalar(count_far[:, :], count[:, :], 1.0, None, ALU.add).then_inc(S["far_prep"], 1)
                    dve.wait_ge(S["far_prep"], 3)
                    dve.tensor_tensor(far[:, 0, :], far[:, 0, :], far[:, 1, :], ALU.mult).then_inc(S["far_prep"], 1)
                    dve.wait_ge(S["far_prep"], 4)
                    dve.sem_inc(S["far_added"], 2)
                    with dve.Fori(0, WINDOWS) as w:
                        dve.wait_ge(S["far_added"], w * 2 + 2)
                        dve.tensor_tensor(far_onehot[:, :, :], each(count_far[:, :]), spread(far[:, 0, :]),
                                          ALU.is_equal).then_inc(S["far_onehot"], 1)
                        dve.wait_ge(S["far_summed"], w + 1)
                        dve.tensor_scalar(count_far[:, :], count_far[:, :], float(WINDOW), None,
                                          ALU.add).then_inc(S["far_added"], 1)
                        add_at(layer, side[0], w * WINDOW, S["far_added"])
                    dve.wait_ge(S["far_added"], 2 * (WINDOWS + 1))
                    reach(dve, S["group_done"], first + g + 1)
                    dve.sem_clear(S["far_added"])
                    dve.sem_clear(S["far_summed"])
                    dve.sem_clear(S["far_prep"])

            def group_step(way, layer, spent, g, k):
                first = 0 if layer is None else way.first(layer)
                origin = 0 if layer is None else way.origin
                u = first + g
                reach(dve, spent, u - 1)
                dve.tensor_tensor(onehot[:, k, :, :], each(count[:, :]), spread(of_group(near, origin + g)),
                                  ALU.is_equal).then_inc(S["onehot_ready"], 1)
                if layer is None:
                    rows = edge_in[:, k, :].rearrange("p (j d) -> p j d", d=ED)
                    high, mid, low = (edge_parts[:, k, part, :, 0:ED] for part in range(PARTS))
                else:
                    rows = gathered[:, k, :, :]
                    high, mid, low = (row_parts[:, k, :, part * D:(part + 1) * D] for part in range(PARTS))
                reach(dve, S["split_high"], u + 1)
                dve.tensor_tensor(rows, rows, high, ALU.subtract).then_inc(S["split_rest"], 1)
                if not (isinstance(g, int) and g == 0):
                    add(layer, first, origin, g - 1, 1 - k)
                    if way.uneven:
                        add_far(layer, first, g - 1)
                reach(dve, S["split_mid"], u + 1)
                dve.tensor_tensor(low, rows, mid, ALU.subtract).then_inc(S["split_low"], 1)

            def last_sums(way, layer):
                first = 0 if layer is None else way.first(layer)
                many = GROUPS if layer is None else way.many
                add(layer, first, 0 if layer is None else way.origin, many - 1, 1)
                if way.uneven:
                    add_far(layer, first, many - 1)
                dve.wait_ge(S["added"], first + many)
                dve.sem_inc(S["sums_done"], 1)

            def split_table(layer, g):
                for c in TABLE_BEFORE.get(g, ()) if isinstance(g, int) else ():
                    n = layer * PER_BATCH + c
                    blocks = slice(c * CHUNK, (c + 1) * CHUNK)
                    dve.wait_ge(S["table_high"], n + 1)
                    dve.tensor_tensor(table_in[c % 2], table_in[c % 2], parts[:, blocks, 0:D],
                                      ALU.subtract).then_inc(S["table_rest"], 1)
                    dve.wait_ge(S["table_mid"], n + 1)
                    dve.tensor_tensor(parts[:, blocks, 2 * D:3 * D], table_in[c % 2], parts[:, blocks, D:2 * D],
                                      ALU.subtract).then_inc(S["table_ready"], 1)

            def add_dense(layer, r, half, windows):
                to = sums_own[0:D, bass.ds((r * 2 + half) * BATCH, BATCH)]
                n = layer * DENSE + half + r * 2
                reach(dve, S["dense_summed"], n + 1)
                reach_alone(dve, S["added"], windows)
                dve.tensor_tensor(to, dense_sum[half][0:D, 0:BATCH], to, ALU.add).then_inc(S["dense_added"], 1)
                dve.wait_ge(S["dense_added"], n * 2 + 1)
                dve.tensor_tensor(to, dense_sum[half][D:2 * D, 0:BATCH], to, ALU.add).then_inc(S["dense_added"], 1)
                reach_alone(dve, S["dense_added"], n * 2 + 2)

            FIRST_ADD = 4

            def dense_behind(layer):
                def behind_of(r, p):
                    windows = EVEN.first(layer) + OPENING + r * PER_ROUND + p
                    if p == (FIRST_ADD if isinstance(r, int) and r == 0 else 1):
                        add_dense(layer, r, 0, windows)
                    if p == PER_BATCH:
                        add_dense(layer, r, 1, windows)
                return behind_of

            def stages(layer):
                base = before(layer)
                ln = before(layer, (LN1, LN2))
                sq = before(layer, (LN1, GCN1, LN2))

                def own_term(m, kind):
                    for k, n, nodes in spots(m, kind):
                        reach_alone(dve, S["deg_held"], n + 1)
                        dve.tensor_tensor(sums_own[D:2 * D, nodes], d_stage[D:2 * D, k, :],
                                          edge_resid[D:2 * D, nodes], ALU.mult).then_inc(S["own_first"], 1)

                def own_next(m, kind):
                    for k, n, nodes in spots(m, kind):
                        reach(dve, S["conv_ready"], base + n + 1)
                        reach(dve, S["deg_held"], base + n + 1)
                        dve.scalar_tensor_tensor(out=sums_own[D:2 * D, nodes], in0=conv[k][D:2 * D, 0:BATCH],
                                                 scalar=0.0, in1=d_stage[D:2 * D, k, :],
                                                 op0=ALU.max, op1=ALU.mult).then_inc(S["own_ready"], 1)

                def inverse_root(m, kind):
                    for k, n, nodes in spots(m, kind):
                        reach(dve, S["deg_held"], base + n + 1)
                        if layer < LN2:
                            reach(dve, S["own_ready"], base + n - 1)
                            reach(dve, S["result_ready"], base + n - 1)
                        else:
                            reach(dve, S["scaled"], sq + n - 1)
                        dve.reciprocal(dinv[:, k, :], d_stage[:, k, :]).then_inc(S["dinv_ready"], 1)

                def residual(m, kind):
                    for k, n, nodes in spots(m, kind):
                        reach(dve, S["conv_ready"], base + n + 1)
                        reach(dve, S["centered"], ln + n - 1)
                        dve.tensor_tensor(r_stage[0:D, k, :], conv[k][D:2 * D, 0:BATCH],
                                          edge_resid[D:2 * D, nodes], ALU.add).then_inc(S["scaled"], 1)

                def norm(k, n):
                    reach(dve, S["var_root"], ln + n + 1)
                    reach(dve, S["dinv_ready"], sq + n + 1)
                    if layer == LN2:
                        reach(dve, S["scaled"], sq + n + 1)
                    dve.reciprocal(d_stage[:, k, :], q_stage[:, k, :]).then_inc(S["rstd_ready"], 1)
                    reach(dve, S["rstd_ready"], ln + n + 1)

                def normalize(m, kind):
                    for k, n, nodes in spots(m, kind):
                        norm(k, n)
                        dve.tensor_tensor(edge_resid[D:2 * D, nodes], conv[k][D:2 * D, 0:BATCH],
                                          d_stage[D:2 * D, k, :], ALU.mult).then_inc(S["new_resid"], 1)
                    for k, n, nodes in spots(m, kind):
                        reach(dve, S["new_resid"], n + 1)
                        reach(dve, S["turned_ready"], base + n - 1)
                        dve.tensor_tensor(h_stage[:, k, :], edge_resid[D:2 * D, nodes], dinv[D:2 * D, k, :],
                                          ALU.mult).then_inc(S["result_ready"], 1)
                        dve.tensor_tensor(sums_own[D:2 * D, nodes], edge_resid[D:2 * D, nodes],
                                          dinv[D:2 * D, k, :], ALU.mult).then_inc(S["own_ready"], 1)

                def scale(m, kind):
                    inverse_root(m, kind)
                    for k, n, nodes in spots(m, kind):
                        reach(dve, S["conv_ready"], base + n + 1)
                        reach(dve, S["dinv_ready"], sq + n + 1)
                        reach(dve, S["squared"], sq + n - 1)
                        dve.tensor_tensor(r_stage[:, k, :], conv[k][:, 0:BATCH], dinv[:, k, :],
                                          ALU.mult).then_inc(S["scaled"], 1)

                def gcn_result(m, kind):
                    for k, n, nodes in spots(m, kind):
                        reach(dve, S["squared"], sq + n + 1)
                        reach(dve, S["turned_ready"], base + n - 1)
                        dve.tensor_tensor(h_stage[:, k, :], q_stage[0:D, k, :], dinv[0:D, k, :],
                                          ALU.mult).then_inc(S["result_ready"], 1)
                        dve.tensor_tensor(sums_own[D:2 * D, nodes], q_stage[D:2 * D, k, :],
                                          dinv[D:2 * D, k, :], ALU.mult).then_inc(S["own_ready"], 1)

                def scale_and_residual(m, kind):
                    inverse_root(m, kind)
                    for k, n, nodes in spots(m, kind):
                        reach(dve, S["conv_ready"], base + n + 1)
                        reach(dve, S["dinv_ready"], sq + n + 1)
                        reach(dve, S["centered"], ln + n - 1)
                        dve.tensor_tensor(d_stage[:, k, :], conv[k][:, 0:BATCH], dinv[:, k, :],
                                          ALU.mult).then_inc(S["scaled_first"], 1)
                        reach(dve, S["scaled_first"], n + 1)
                        dve.scalar_tensor_tensor(out=r_stage[0:D, k, :], in0=d_stage[D:2 * D, k, :],
                                                 scalar=bias[D:2 * D, 1:2], in1=edge_resid[D:2 * D, nodes],
                                                 op0=ALU.add, op1=ALU.add).then_inc(S["scaled"], 1)

                def last_result(m, kind):
                    for k, n, nodes in spots(m, kind):
                        norm(k, n)
                        reach(dve, S["turned_ready"], base + n - 1)
                        dve.tensor_tensor(h_stage[:, k, :], conv[k][0:D, 0:BATCH], d_stage[0:D, k, :],
                                          ALU.mult).then_inc(S["result_ready"], 1)

                return {0: {1: own_term, 2: own_next},
                        1: {1: own_next},
                        LN1: {1: residual, 2: inverse_root, 3: normalize},
                        GCN1: {1: scale, 2: gcn_result},
                        LN2: {1: scale_and_residual, 4: last_result}}[layer]

            is_uneven = dve.value_load(uneven[0:1, 0:1], min_val=0, max_val=1)
            with dve.If(is_uneven > 0):
                dve.wait_ge(S["zeroed"], 2)
                dve.wait_ge(S["matrix_cleared"], 16 * PIECES * AHEAD)
                all_pairs(dve, lambda g, k: group_step(UNEVEN, None, S["group_done"], g, k), 0, GROUPS // 2)
                last_sums(UNEVEN, None)
                for layer in range(LAYERS):
                    if layer:
                        dve.wait_ge(S["cleared_sums"], layer * BATCHES)
                    all_pairs(dve, lambda g, k: group_step(UNEVEN, layer, S["group_done"], g, k), 0, GROUPS // 2)
                    last_sums(UNEVEN, layer)
                    whole_phase(dve, stages(layer))
            with dve.If(is_uneven < 1):
                dve.wait_ge(S["zeroed"], 2)
                all_pairs(dve, lambda g, k: group_step(EVEN, None, S["summed"], g, k), 0, GROUPS // 2)
                last_sums(EVEN, None)
                dve.wait_ge(S["matrix_cleared"], 16 * PIECES * DENSE)
                for layer in range(LAYERS):
                    if layer:
                        dve.wait_ge(S["cleared_sums"], layer * BATCHES)

                    def group(g, k, r, p):
                        split_table(layer, g)
                        group_step(EVEN, layer, S["summed"], g, k)

                    propagate(dve, group, stages(layer), behind=dense_behind(layer))
                    last_sums(EVEN, layer)
                    finish(stages(layer))

        @block.tensor
        def _(pe):
            pe.wait_ge(S["const"], 11)

            def turn_x(pair):
                for k in range(2):
                    batch = pair * 2 + k
                    last = isinstance(pair, int) and (batch + 1) * BATCH > N
                    reach_alone(pe, x_landed[k], pair * 32 + (64 if last else 32))
                    reach_alone(pe, S["x_taken"], batch - 1)
                    for q in range(TURNS):
                        ins = pe.transpose(conv[k][:, q * TURN:(q + 1) * TURN],
                                           x_in[:, k, q, :, :].rearrange("p h d -> p (h d)"), ident[0:TURN, 0:TURN])
                    ins.then_inc(S["x_turned"], 1)

            turn_x(0)
            rounds(pe, turn_x, 1, BATCHES // 2 - 1)
            turn_x(BATCHES // 2 - 1)
            pe.wait_ge(S["x_taken"], BATCHES)
            pe.wait_ge(S["weights_in"], 16 * WEIGHT_LOADS)
            pe.wait_ge(S["row_done"], 2)
            pe.wait_ge(S["uneven_ready"], 1)

            def of_parts(layer, k, j, part):
                if layer is None:
                    return edge_parts[:, k, part, j, :]
                return row_parts[:, k, j, part * D:(part + 1) * D]

            def sum_tiles(layer, bank, k, hot):
                held = EXTRA if layer is None else D
                for j in range(TILES):
                    for part in range(PARTS):
                        ins = pe.matmul(bank[0:held, 0:WINDOW], of_parts(layer, k, j, part), hot[:, j, :],
                                        start=(j == 0 and part == 0), stop=(j == TILES - 1 and part == PARTS - 1))
                return ins

            def sum_far(layer, first, g, k):
                wide = pe.value_load(wide_row[0:1, bass.ds(g, 1)], min_val=0, max_val=1)
                with pe.If(wide > 0):
                    with pe.Fori(0, WINDOWS) as w:
                        pe.wait_ge(S["far_onehot"], w + 1)
                        sum_tiles(layer, side[0], k, far_onehot[:, :, :]).then_inc(S["far_summed"], 1)
                    pe.wait_ge(S["far_summed"], WINDOWS)
                    pe.sem_clear(S["far_onehot"])
                reach(pe, S["summed"], first + g + 1)
                pe.sem_inc(S["group_done"], 1)

            def sums(way, layer, g, k):
                first = 0 if layer is None else way.first(layer)
                reach(pe, S["onehot_ready"], first + g + 1)
                reach(pe, S["added"], first + g - 1)
                reach(pe, S["split_low"], first + g + 1)
                sum_tiles(layer, window[k], k, onehot[:, k, :, :]).then_inc(S["summed"], 1)
                if way.uneven:
                    sum_far(layer, first, g, k)

            def dense(layer):
                def dense_chunk(r, p):
                    if not has_chunk(r, p):
                        return
                    batch, c = divmod(p, PER_BATCH)
                    half = 0 if r is None else 1 - batch
                    slot = chunk_slot(r, p)
                    if r is None:
                        reach(pe, S["table_ready"], layer * PER_BATCH + c + 1)
                    reach_alone(pe, counts_landed[slot], chunk_landings(layer, r, p) * 16 + 16)
                    if c == 0:
                        added = (layer * DENSE - 1) * 2 + (0 if r is None else (batch + 1) * 2 + r * 4)
                        reach_alone(pe, S["dense_added"], added)
                    for i in range(CHUNK):
                        block = c * CHUNK + i
                        opens = c == 0 and i == 0
                        closes = c == PER_BATCH - 1 and i == CHUNK - 1
                        for low in (True, False) if closes else (False, True):
                            if low:
                                ins = pe.matmul(dense_sum[half][0:D, 0:BATCH], parts[:, block, 2 * D:3 * D],
                                                counts[:, slot, i, :], start=False, stop=False)
                            else:
                                ins = pe.matmul(dense_sum[half][:, 0:BATCH], parts[:, block, 0:2 * D],
                                                counts[:, slot, i, :], start=opens, stop=closes)
                    ins.then_inc(S["counts_used"], 1)
                    if c == PER_BATCH - 1:
                        pe.wait_ge(S["counts_used"], chunk_number(layer, r, p) + 1)
                        pe.sem_inc(S["dense_summed"], 1)
                return dense_chunk

            def stages(way, layer):
                base = before(layer)
                ln = before(layer, (LN1, LN2))
                sq = before(layer, (LN1, GCN1, LN2))

                def gate(m, kind):
                    if way.uneven:
                        return
                    if kind == 0:
                        reach(pe, S["added"], EVEN.first(layer) + OPENING + m * PER_ROUND)
                        reach(pe, S["dense_added"], (layer * DENSE + 2) * 2 + m * 4)
                    elif not (isinstance(m, int) and m == ROUNDS - 1):
                        reach(pe, S["added"], EVEN.first(layer) + OPENING + (m + 1) * PER_ROUND + SLACK)

                def degree(k, n, nodes):
                    reach_alone(pe, S["rows_ready"], base + n - 1)
                    pe.matmul(side[k][:, 0:BATCH], deg_row[:, :], edge_resid[0:EXTRA, nodes],
                              start=True, stop=True).then_inc(S["deg_ready"], 1)

                def degrees(m, kind):
                    for k, n, nodes in spots(m, kind):
                        degree(k, n, nodes)

                def convolve(m, kind):
                    gate(m, kind)
                    for k, n, nodes in spots(m, kind):
                        if layer == 0:
                            reach(pe, S["own_first"], n + 1)
                        if layer < LN1:
                            reach(pe, S["own_ready"], base + n - 1)
                        if layer == GCN1:
                            reach(pe, S["scaled"], sq + n - 1)
                        elif layer == LN1:
                            reach(pe, S["new_resid"], n - 1)
                        else:
                            reach(pe, S["result_ready"], base + n - 1)
                        last = pe.matmul(conv[k][:, 0:BATCH], weights[:, layer, :], sums_own[:, nodes],
                                         start=True, stop=(layer >= GCN1))
                        if layer < GCN1:
                            last = pe.matmul(conv[k][:, 0:BATCH], edge_w[:, layer, :], edge_resid[0:EXTRA, nodes],
                                             start=False, stop=True)
                        last.then_inc(S["conv_ready"], 1)

                def degrees_and_convolve(m, kind):
                    degrees(m, kind)
                    convolve(m, kind)

                def centre(m, kind):
                    for k, n, nodes in spots(m, kind):
                        reach(pe, S["scaled"], sq + n + 1)
                        pe.matmul(conv[k][:, 0:BATCH], center[:, :], r_stage[0:D, k, :],
                                  start=True, stop=True).then_inc(S["centered"], 1)
                        if layer == LN1:
                            degree(k, n, nodes)

                def variance(m, kind):
                    for k, n, nodes in spots(m, kind):
                        reach(pe, S["squared"], sq + n + 1)
                        reach(pe, S["deg_held"], base + n + 1)
                        pe.matmul(side[k][:, 0:BATCH], mean[:, :], q_stage[0:D, k, :],
                                  start=True, stop=True).then_inc(S["variance"], 1)

                def turn_result(m, kind):
                    for k, n, nodes in spots(m, kind):
                        reach_alone(pe, S["result_ready"], base + n + 1)
                        for q in range(TURNS):
                            ins = pe.transpose(side[k][0:TURN, q * D:(q + 1) * D], h_stage[:, k, q * TURN:(q + 1) * TURN],
                                               ident[0:D, 0:D])
                        ins.then_inc(S["turned_ready"], 1)

                return {0: {0: degrees, 2: convolve, 3: turn_result},
                        1: {0: degrees_and_convolve, 2: turn_result},
                        LN1: {0: convolve, 1: centre, 2: variance, 4: turn_result},
                        GCN1: {0: degrees_and_convolve, 3: turn_result},
                        LN2: {0: degrees_and_convolve, 2: centre, 3: variance, 5: turn_result}}[layer]

            def opening(layer):
                if layer:
                    pe.wait_ge(S["own_ready"], before(layer))
                    pe.wait_ge(S["result_ready"], before(layer))
                else:
                    pe.wait_ge(S["sums_done"], 1)

            is_uneven = pe.value_load(uneven[0:1, 0:1], min_val=0, max_val=1)
            with pe.If(is_uneven > 0):
                all_pairs(pe, lambda g, k: sums(UNEVEN, None, g, k), 0, GROUPS // 2)
                for layer in range(LAYERS):
                    opening(layer)
                    reach(pe, S["rows_ready"], before(layer))
                    all_pairs(pe, lambda g, k: sums(UNEVEN, layer, g, k), 0, GROUPS // 2)
                    pe.wait_ge(S["sums_done"], layer + 2)
                    whole_phase(pe, stages(UNEVEN, layer))
            with pe.If(is_uneven < 1):
                all_pairs(pe, lambda g, k: sums(EVEN, None, g, k), 0, GROUPS // 2)
                for layer in range(LAYERS):
                    opening(layer)
                    chunk = dense(layer)

                    def group(g, k, r, p):
                        for c in TABLE_BEFORE.get(g, ()) if isinstance(g, int) else ():
                            chunk(None, c)
                        sums(EVEN, layer, g, k)

                    propagate(pe, group, stages(EVEN, layer), behind=chunk)
                    pe.wait_ge(S["sums_done"], layer + 2)
                    finish(stages(EVEN, layer))


WEIGHT_LOADS = 2 * (3 * 4 + 2 * 3)

_INS = ["x", "src", "dst", "edge_attr_16"] + [f"L0_gnn_{n}{i}" for i in (1, 2, 3) for n in "Wb"] \
    + [f"L1_gnn_{n}{i}" for i in (1, 2) for n in "Wb"]


def kernel(**inputs):
    import numpy as _np
    import concourse.bacc as _bacc
    from concourse import mybir as _mybir
    from concourse.bass_utils import run_bass_kernel_spmd as _run

    nc = _bacc.Bacc("TRN2", target_bir_lowering=False, num_devices=1)
    arrays, args = {}, []
    for name in _INS:
        a = _np.ascontiguousarray(inputs[name])
        arrays[f"in_{name}_dram"] = a
        args.append(nc.dram_tensor(f"in_{name}_dram", a.shape, _mybir.dt.from_np(a.dtype), kind="ExternalInput").ap())
    out = nc.dram_tensor("out_dram", inputs["x"].shape, _mybir.dt.float32, kind="ExternalOutput").ap()
    bass_gnn_resnorm(nc, *args[:4], args[4::2], args[5::2], out)
    r = _run(nc, [arrays], core_ids=[0])
    return r.results[0]["out_dram"]
```
